# Optimizing a Trainium2 kernel written in Bass

```python
import numpy as np
import jax
import jax.numpy as jnp

def _softmax(x, axis=-1):
    return jax.nn.softmax(x, axis=axis)

def _gelu(x):
    return jax.nn.gelu(x, approximate=True)

def _silu(x):
    return jax.nn.silu(x)

def _sigmoid(x):
    return jax.nn.sigmoid(x)

def _layernorm(x, axis=-1, eps=1e-05):
    m = jnp.mean(x, axis=axis, keepdims=True)
    v = jnp.var(x, axis=axis, keepdims=True)
    return (x - m) / jnp.sqrt(v + eps)

def _scatter_add(tgt, idx, src, axis=0):
    return tgt.at[idx].add(src)

def _segment_sum(src, seg, n):
    return jax.ops.segment_sum(src, seg, n)
kernel_name = 'mk_seq_postln_d1_jaxref_r8_743b20'

def setup_inputs(seed: int=0):
    np.random.seed(seed)
    _w = jnp.asarray

    def _L0_attn_setup():
        import jax, jax.numpy as jnp
        import numpy as np
        B, S, D = (2, 128, 512)
        H, KVH, HD = (32, 8, 128)
        GROUPS = H // KVH
        LAT, LH = (128, 32)
        THETA = 10000.0
        SCALE = 1.0 / float(np.sqrt(HD))

        def _rope_cos_sin(seq_len, head_dim, theta):
            inv_freq = 1.0 / theta ** (jnp.arange(0, head_dim, 2, dtype=jnp.float32) / head_dim)
            t = jnp.arange(seq_len, dtype=jnp.float32)
            freqs = jnp.outer(t, inv_freq)
            emb = jnp.concatenate([freqs, freqs], axis=-1)
            return (jnp.cos(emb), jnp.sin(emb))

        def _rotate_half(x):
            h = x.shape[-1] // 2
            return jnp.concatenate([-x[..., h:], x[..., :h]], axis=-1)

        def _apply_rope(x, cos, sin):
            return x * cos[None, None] + _rotate_half(x) * sin[None, None]

        def _causal_attn(q, k, v, scale):
            s = jnp.einsum('bhqd,bhkd->bhqk', q, k) * scale
            mask = jnp.tril(jnp.ones((q.shape[2], k.shape[2]), dtype=bool))
            s = jnp.where(mask[None, None], s, jnp.finfo(s.dtype).min)
            p = jax.nn.softmax(s, axis=-1)
            return jnp.einsum('bhqk,bhkd->bhqd', p, v)
        key = jax.random.key(seed)
        ks = jax.random.split(key, 9)
        sd = 0.02
        mk = lambda k, shape: jax.random.normal(k, shape, dtype=jnp.float32) * sd
        return {'hidden_states': jax.random.normal(ks[0], (B, S, D), dtype=jnp.float32), 'w_q': mk(ks[1], (D, H * HD)), 'w_k': mk(ks[2], (D, KVH * HD)), 'w_v': mk(ks[3], (D, KVH * HD)), 'w_o': mk(ks[4], (H * HD, D)), 'w_lq': mk(ks[5], (D, LAT)), 'w_lk': mk(ks[6], (LAT, LH * HD)), 'w_lv': mk(ks[7], (D, LH * HD)), 'w_lo': mk(ks[8], (LH * HD, D))}
    _L0_attn_in = _L0_attn_setup()

    def _L0_ffn_setup():
        import jax, jax.numpy as jnp
        import numpy as np
        R = 16
        LORA_ALPHA = 16
        SCALING = LORA_ALPHA / R
        key = jax.random.key(seed)
        kx, kr, ka = jax.random.split(key, 3)
        B, S, D, DO, E = (4, 256, 512, 512, 8)
        x = jax.random.normal(kx, (B, S, D), dtype=jnp.float32)
        bound_r = 1.0 / np.sqrt(D)
        route_w = jax.random.uniform(kr, (E, D), jnp.float32, -bound_r, bound_r)
        bound_a = 1.0 / np.sqrt(D)
        A = jax.random.uniform(ka, (E, R, D), jnp.float32, -bound_a, bound_a)
        kb = jax.random.fold_in(key, 7)
        Bw = jax.random.normal(kb, (E, DO, R), dtype=jnp.float32) * 0.02
        return {'x': x, 'route_w': route_w, 'A': A, 'Bw': Bw}
    _L0_ffn_in = _L0_ffn_setup()
    _d = {'L0_attn_hidden_states': _L0_attn_in['hidden_states'], 'L0_attn_w_q': _L0_attn_in['w_q'], 'L0_attn_w_k': _L0_attn_in['w_k'], 'L0_attn_w_v': _L0_attn_in['w_v'], 'L0_attn_w_o': _L0_attn_in['w_o'], 'L0_attn_w_lq': _L0_attn_in['w_lq'], 'L0_attn_w_lk': _L0_attn_in['w_lk'], 'L0_attn_w_lv': _L0_attn_in['w_lv'], 'L0_attn_w_lo': _L0_attn_in['w_lo'], 'L0_ffn_route_w': _L0_ffn_in['route_w'], 'L0_ffn_A': _L0_ffn_in['A'], 'L0_ffn_Bw': _L0_ffn_in['Bw']}
    _x0 = _d['L0_attn_hidden_states']
    _d['L0_attn_hidden_states'] = jax.random.normal(jax.random.fold_in(jax.random.key(seed), 1), (1, 1024, 512), dtype=_x0.dtype)
    del _x0
    return _d

def reference(L0_attn_hidden_states, L0_attn_w_q, L0_attn_w_k, L0_attn_w_v, L0_attn_w_o, L0_attn_w_lq, L0_attn_w_lk, L0_attn_w_lv, L0_attn_w_lo, L0_ffn_route_w, L0_ffn_A, L0_ffn_Bw):

    def _L0_attn_ref(hidden_states, w_q, w_k, w_v, w_o, w_lq, w_lk, w_lv, w_lo):
        import jax, jax.numpy as jnp
        import numpy as np
        B, S, D = (2, 128, 512)
        H, KVH, HD = (32, 8, 128)
        GROUPS = H // KVH
        LAT, LH = (128, 32)
        THETA = 10000.0
        SCALE = 1.0 / float(np.sqrt(HD))

        def _rope_cos_sin(seq_len, head_dim, theta):
            inv_freq = 1.0 / theta ** (jnp.arange(0, head_dim, 2, dtype=jnp.float32) / head_dim)
            t = jnp.arange(seq_len, dtype=jnp.float32)
            freqs = jnp.outer(t, inv_freq)
            emb = jnp.concatenate([freqs, freqs], axis=-1)
            return (jnp.cos(emb), jnp.sin(emb))

        def _rotate_half(x):
            h = x.shape[-1] // 2
            return jnp.concatenate([-x[..., h:], x[..., :h]], axis=-1)

        def _apply_rope(x, cos, sin):
            return x * cos[None, None] + _rotate_half(x) * sin[None, None]

        def _causal_attn(q, k, v, scale):
            s = jnp.einsum('bhqd,bhkd->bhqk', q, k) * scale
            mask = jnp.tril(jnp.ones((q.shape[2], k.shape[2]), dtype=bool))
            s = jnp.where(mask[None, None], s, jnp.finfo(s.dtype).min)
            p = jax.nn.softmax(s, axis=-1)
            return jnp.einsum('bhqk,bhkd->bhqd', p, v)
        x = hidden_states
        bsz, q_len, _ = x.shape
        q = (x @ w_q).reshape(bsz, q_len, H, HD).transpose(0, 2, 1, 3)
        k = (x @ w_k).reshape(bsz, q_len, KVH, HD).transpose(0, 2, 1, 3)
        v = (x @ w_v).reshape(bsz, q_len, KVH, HD).transpose(0, 2, 1, 3)
        lq = x @ w_lq
        lk = (lq @ w_lk).reshape(bsz, q_len, LH, HD).transpose(0, 2, 1, 3)
        lv = (x @ w_lv).reshape(bsz, q_len, LH, HD).transpose(0, 2, 1, 3)
        cos, sin = _rope_cos_sin(q_len, HD, THETA)
        q = _apply_rope(q, cos, sin)
        k = _apply_rope(k, cos, sin)
        lk = _apply_rope(lk, cos, sin)
        k = jnp.repeat(k, GROUPS, axis=1)
        v = jnp.repeat(v, GROUPS, axis=1)
        attn = _causal_attn(q, k, v, SCALE)
        lat = _causal_attn(q, lk, lv, SCALE)
        attn = attn.transpose(0, 2, 1, 3).reshape(bsz, q_len, H * HD)
        lat = lat.transpose(0, 2, 1, 3).reshape(bsz, q_len, LH * HD)
        return attn @ w_o + lat @ w_lo

    def _L0_ffn_ref(x, route_w, A, Bw):
        import jax, jax.numpy as jnp
        import numpy as np
        R = 16
        LORA_ALPHA = 16
        SCALING = LORA_ALPHA / R
        logits = jnp.einsum('bsd,ed->bse', x, route_w)
        topk_v, topk_idx = jax.lax.top_k(logits, 1)
        E = logits.shape[-1]
        route_weight = jax.nn.one_hot(topk_idx[..., 0], E, dtype=logits.dtype) * topk_v
        h = jnp.einsum('bsd,erd->bser', x, A)
        wh = route_weight[..., None] * h
        out = jnp.einsum('bser,eor->bso', wh, Bw) * SCALING
        return out
    x = L0_attn_hidden_states
    x = _layernorm(x + _L0_attn_ref(x, L0_attn_w_q, L0_attn_w_k, L0_attn_w_v, L0_attn_w_o, L0_attn_w_lq, L0_attn_w_lk, L0_attn_w_lv, L0_attn_w_lo), axis=-1)
    x = _layernorm(x + _L0_ffn_ref(x, L0_ffn_route_w, L0_ffn_A, L0_ffn_Bw), axis=-1)
    return x

_drawn_inputs = setup_inputs


def setup_inputs(seed=0):
    import zlib

    import numpy as np

    out = dict(_drawn_inputs(seed))
    spreads = {}
    factors = {'L0_attn_w_q': 5.613, 'L0_attn_w_k': 5.72, 'L0_attn_w_lq': 8.0, 'L0_attn_w_lk': 8.0}
    for name, (base, spread) in spreads.items():
        noise = np.random.default_rng([zlib.crc32(name.encode()), seed]).standard_normal(out[name].shape)
        drawn = base * np.exp(spread * noise) if base else spread * noise
        out[name] = jnp.asarray(drawn.astype(out[name].dtype))
    for name, factor in factors.items():
        out[name] = (out[name] * factor).astype(out[name].dtype)
    return out
```

```python
from contextlib import ExitStack

import numpy as np

import concourse.bass as bass
from concourse import mybir

P = 128
F32 = mybir.dt.float32
F32R = mybir.dt.float32r
BF16 = mybir.dt.bfloat16
ALU = mybir.AluOpType
ACT = mybir.ActivationFunctionType
AX = mybir.AxisListType

S, D = 1024, 512
H, KVH, HD = 32, 8, 128
E, R = 8, 16
GROUPS = KVH
PAIRS = 2
CT = D // P
ST = S // P
HALF = HD // 2
EPS = 1e-5
MASKED = -1e30

STEPS = 4
TILES = STEPS * ST
CHUNKS = TILES // 2
T_LAG = 3
P_BUFS = 4
RAW_SLOTS = 3
SEED = 1
RAW_COLS = 1024

LOADS = ("q0", "kv", "lv0", "oa0", "ob0", "q1", "lv1", "oa1", "ob1")
POOL_LO = ("q0", "kv", "lv0", "q1", "lv1")
DVE_LO = ("oa0", "ob0", "oa1", "ob1")

UNITS = (
    [x for t in range(ST) for x in (("ql", t), ("kv", t))] + [("lv", x) for x in range(ST // 2)],
    [("ql", t) for t in range(ST)] + [("lv", x) for x in range(ST // 2)],
)
ROPES = tuple(sum(k != "lv" for k, _ in u) for u in UNITS)
LN_TILES = ST // 2
BANKS = 4


def blocks_of(tile):
    i = tile % ST
    return [(0, min(i, 3) + 1)] + ([(4, i + 1)] if i > 3 else [])


UNITS_BEFORE = [sum(len(blocks_of(t)) for t in range(n)) for n in range(TILES + 1)]
T_UNITS = UNITS_BEFORE[-1]


def pieces_of(i):
    w = P * (i + 1)
    if w <= 512:
        return [(0, w, 0)]
    first = 384 if w == 640 else 512
    return [(512 - first, first, 0), (512, w - first, first)]


def block_kernel(nc, xT, x, wlq, wq, wkv, wlk, wlv, wo, cos, sin, route_a, bwT, out):
    with ExitStack() as ctx:
        def sb(name, shape, dt=F32):
            return ctx.enter_context(nc.sbuf_tensor(name, shape, dt))

        def sem(name):
            return ctx.enter_context(nc.semaphore(name))

        ps = ctx.enter_context(nc.psum_tensor("ps", [P, 8, 512], F32))

        x_hi, x_lo = sb("x_hi", [P, CT, S], F32R), sb("x_lo", [P, CT, S], F32R)
        lq_hi, lq_lo = sb("lq_hi", [P, S], F32R), sb("lq_lo", [P, S], F32R)
        k_hi, k_lo = sb("k_hi", [P, S], F32R), sb("k_lo", [P, S], F32R)
        v_hi, v_lo = sb("v_hi", [P, ST, HD], F32R), sb("v_lo", [P, ST, HD], F32R)
        ql_hi, ql_lo = sb("ql_hi", [P, 4, S], F32R), sb("ql_lo", [P, 4, S], F32R)
        lv_hi, lv_lo = sb("lv_hi", [P, 2, ST, HD], F32R), sb("lv_lo", [P, 2, ST, HD], F32R)
        o_hi, o_lo = sb("o_hi", [P, 2, S], F32R), sb("o_lo", [P, 2, S], F32R)
        pt_hi, pt_lo = sb("pt_hi", [P, 2, ST * 256], F32R), sb("pt_lo", [P, 2, ST * 256], F32R)
        wlk_raw = sb("wlk_raw", [P, 256])
        wlk_hi, wlk_lo = sb("wlk_hi", [P, 256], F32R), sb("wlk_lo", [P, 256], F32R)
        raw = sb("raw", [P, RAW_SLOTS, RAW_COLS])
        probs = sb("probs", [P, P_BUFS, S])
        acc = sb("acc", [P, ST, D])
        cos_sb, sin_sb = sb("cos_sb", [P, ST, HALF]), sb("sin_sb", [P, ST, HALF])
        ident = sb("ident", [P, P])
        ident_b, mask_b = sb("ident_b", [P, P], BF16), sb("mask_b", [P, P], BF16)
        neg_max, row_sum, inv_sum = sb("neg_max", [P, 4]), sb("row_sum", [P, 4]), sb("inv_sum", [P, 4])
        stats = sb("stats", [P, ST, 8])
        rstd, ve, root, newton = (sb(n, [P, ST]) for n in ("rstd", "ve", "root", "newton"))
        order = sb("order", [P, E])
        route = sb("route", [P, 5, ST, E])
        top = sb("top", [P, ST])
        top2 = sb("top2", [P, ST])

        def parts(name):
            half, at, n = {"q": (1, 0, 1024), "kv": (1, 1024, 1024), "lv": (0, 0, 1024),
                           "oa": (0, 0, 1024), "ob": (0, 1024, 1024)}[name.rstrip("01")]
            return pt_hi[:, half, at:at + n], pt_lo[:, half, at:at + n]

        q_w = [p.rearrange("p (c n) -> p c n", c=CT) for p in parts("q")]
        kv_w = [p.rearrange("p (c n) -> p c n", c=CT) for p in parts("kv")]
        lv_w = [p.rearrange("p (c n) -> p c n", c=CT) for p in parts("lv")]
        o_w = [t[:, 0, :].rearrange("p (s n) -> p s n", s=STEPS) for t in (pt_hi, pt_lo)]

        names = """x_in tab_in wlq_in res_in wlk_in ffn_in const_made x_hi_made x_lo_made wlq_hi_made wlq_lo_made
            lq_mm lq_hi_made lq_lo_made w_hi w_lo_pool w_lo_dve wlk_hi_made wlk_lo_made
            ql_mm kv_mm lv_mm v_hi_made v_lo_made lv_hi_made lv_lo_made
            rope_mul rope_add rope_t rope_hi rope_lo
            scored maxed exped inverted normed turned pt_hi_made pt_lo_made pv_mm o_hi_made o_lo_made
            out_mm out_added ln_chain x1_made x1_turned x1T_made logits_mm route_chain wh_made wh_turned whT_made
            y_mm y_added ln2_chain ve_made root_made ve2_made root2_made finished stored""".split()
        q = {n: sem(n) for n in names}
        raw_in = [sem(f"raw_in{i}") for i in range(RAW_SLOTS)]

        def per_pair(g, pair, n, k):
            return g * (PAIRS * n) + (pair * n + k)

        def rope_base(g, pair, k):
            return g * sum(ROPES) + (pair * ROPES[0] + k)

        def load_landed(eng, g, name):
            i = LOADS.index(name)
            per_slot = len(LOADS) // RAW_SLOTS
            eng.wait_ge(raw_in[i % RAW_SLOTS], g * (16 * per_slot) + 16 * (i // RAW_SLOTS + 1))

        def raw_of(name):
            return raw[:, LOADS.index(name) % RAW_SLOTS, :]

        block = ctx.enter_context(nc.Block())

        @block.sync
        def _(sp):
            sp.dma_start(acc[:].rearrange("p t n -> p (t n)"), xT).then_inc(q["x_in"], 16)
            sp.dma_start(probs[:, 0, 0:512], wlq).then_inc(q["wlq_in"], 16)
            sp.dma_start(cos_sb[:], cos).then_inc(q["tab_in"], 16)
            sp.dma_start(sin_sb[:], sin).then_inc(q["tab_in"], 16)
            sp.wait_ge(q["x_lo_made"], CT)
            sp.dma_start(acc[:], x).then_inc(q["res_in"], 16)
            with sp.Fori(0, GROUPS) as g:
                for pair in range(PAIRS):
                    sp.wait_ge(q["wlk_lo_made"], SEED + per_pair(g, pair, 1, 0))
                    sp.dma_start(wlk_raw[:], wlk[g, pair]).then_inc(q["wlk_in"], 16)
                    for i, name in enumerate(LOADS):
                        if (i >= LOADS.index("q1")) != bool(pair):
                            continue
                        before = LOADS[i - RAW_SLOTS]
                        now = int(i >= RAW_SLOTS)
                        if before in POOL_LO:
                            n = POOL_LO.index(before) + 1
                            sp.wait_ge(q["w_lo_pool"], SEED + g * len(POOL_LO) + (n if now else 0))
                        else:
                            n = DVE_LO.index(before) + 1
                            sp.wait_ge(q["w_lo_dve"], SEED + g * len(DVE_LO) + (n if now else 0))
                        kind = name.rstrip("01")
                        src = {"q": lambda: wq[g, pair], "kv": lambda: wkv[g], "lv": lambda: wlv[g, pair],
                               "oa": lambda: wo[g, pair, 0], "ob": lambda: wo[g, pair, 1]}[kind]()
                        sp.dma_start(raw_of(name), src).then_inc(raw_in[i % RAW_SLOTS], 16)
            sp.wait_ge(q["w_lo_dve"], SEED + GROUPS * len(DVE_LO))
            sp.wait_ge(q["w_lo_pool"], SEED + GROUPS * len(POOL_LO))
            sp.dma_start(raw[:, 0, 0:CT * (E + E * R)], route_a).then_inc(q["ffn_in"], 16)
            sp.dma_start(raw[:, 1, 0:D], bwT).then_inc(q["ffn_in"], 16)
            for t in range(ST):
                sp.wait_ge(q["finished"], t + 1)
                sp.dma_start(out[:, t, :], acc[:, t, :]).then_inc(q["stored"], 16)
            sp.wait_ge(q["stored"], 16 * ST)

        @block.tensor
        def _(pe):
            def three(dst, hi_lo_a, hi_lo_b, first, last=False):
                (ah, al), (bh, bl) = hi_lo_a, hi_lo_b
                pe.matmul(dst, ah, bh, start=first, stop=False, skip_group_check=True)
                pe.matmul(dst, ah, bl, start=False, stop=False, skip_group_check=True)
                return pe.matmul(dst, al, bh, start=False, stop=last, skip_group_check=True)

            def x_tile(c, t):
                return [a[:, c, P * t:P * t + P] for a in (x_hi, x_lo)]

            def latent_query():
                pe.wait_ge(q["x_lo_made"], CT)
                pe.wait_ge(q["wlq_lo_made"], 1)
                for n in range(2):
                    for c in range(CT):
                        mm = three(ps[:, 4 + n, :],
                                   [a[:, 0, P * c:P * c + P] for a in (pt_hi, pt_lo)],
                                   [a[:, c, 512 * n:512 * n + 512] for a in (x_hi, x_lo)], c == 0, c == CT - 1)
                    mm.then_inc(q["lq_mm"], 1)

            def unit(g, pair, u):
                kind, t = UNITS[pair][u]
                bank = 4 + u % BANKS
                if u >= BANKS:
                    k0, t0 = UNITS[pair][u - BANKS]
                    if k0 == "ql":
                        n = sum(k != "lv" for k, _ in UNITS[pair][:u - BANKS + 1])
                        pe.wait_ge(q["rope_mul"], rope_base(g, pair, n))
                    elif k0 == "kv":
                        pe.wait_ge(q["v_lo_made"], g * ST + (t0 + 1))
                if kind == "ql":
                    if t == 0:
                        pe.wait_ge(q["w_lo_pool"], SEED + g * len(POOL_LO) + (POOL_LO.index(f"q{pair}") + 1))
                        pe.wait_ge(q["wlk_lo_made"], SEED + per_pair(g, pair, 1, 1))
                    for c in range(CT):
                        three(ps[:, bank, 0:256], x_tile(c, t), [w[:, c, :] for w in q_w], c == 0)
                    three(ps[:, bank, 256:512], [a[:, P * t:P * t + P] for a in (lq_hi, lq_lo)],
                          [wlk_hi[:], wlk_lo[:]], False, True).then_inc(q["ql_mm"], 1)
                elif kind == "kv":
                    if t == 0:
                        pe.wait_ge(q["w_lo_pool"], SEED + g * len(POOL_LO) + (POOL_LO.index("kv") + 1))
                    for c in range(CT):
                        mm = three(ps[:, bank, 0:256], x_tile(c, t), [w[:, c, :] for w in kv_w], c == 0, c == CT - 1)
                    mm.then_inc(q["kv_mm"], 1)
                else:
                    if t == 0:
                        pe.wait_ge(q["w_lo_pool"], SEED + g * len(POOL_LO) + (POOL_LO.index(f"lv{pair}") + 1))
                    for y in range(2):
                        for c in range(CT):
                            mm = three(ps[:, bank, 256 * y:256 * y + 256], x_tile(c, 2 * t + y),
                                       [w[:, c, :] for w in lv_w], c == 0 and y == 0, c == CT - 1 and y == 1)
                    mm.then_inc(q["lv_mm"], 1)

            def turn_roped(g, pair, r):
                pe.wait_ge(q["rope_add"], rope_base(g, pair, r + 1))
                if r == 0:
                    pe.wait_ge(q["out_added"], SEED + per_pair(g, pair, ST, 0))
                else:
                    if r >= 2:
                        pe.wait_ge(q["rope_lo"], rope_base(g, pair, r - 1))
                n = 4 if UNITS[pair][r][0] == "ql" else 1
                for b in range(n):
                    mm = pe.transpose(ps[:, r % 2, P * b:P * b + P], probs[:, r % P_BUFS, P * b:P * b + P], ident[:])
                mm.then_inc(q["rope_t"], 1)

            def scores(g, pair, n):
                step, i = divmod(n, ST)
                a, latent = divmod(step, 2)
                if n == 0:
                    pe.wait_ge(q["rope_lo"], rope_base(g, pair, ROPES[pair]))
                if n >= 2:
                    pe.wait_ge(q["exped"], per_pair(g, pair, TILES, n - 1))
                b0 = 2 * (n % 2)
                keys = (ql_hi[:, 2 + a, :], ql_lo[:, 2 + a, :]) if latent else (k_hi[:], k_lo[:])
                lhs = [w[:, a, P * i:P * i + P] for w in (ql_hi, ql_lo)]
                bank = ps[:, b0:b0 + 2, :].rearrange("p b n -> p (b n)")
                pieces = pieces_of(i)
                for hl in range(3):
                    for at, w, k0 in pieces:
                        pe.matmul(bank[:, at:at + w], lhs[hl == 2], keys[hl == 1][:, k0:k0 + w],
                                  start=hl == 0, stop=False, skip_group_check=True)
                end = pieces[-1][0] + pieces[-1][1]
                pe.matmul(bank[:, end - P:end], ident_b[:], mask_b[:], start=False, stop=True,
                          skip_group_check=True).then_inc(q["scored"], 1)

            def turn_probs(g, pair, n):
                pe.wait_ge(q["normed"], per_pair(g, pair, TILES, n + 1))
                for x, (b0, b1) in enumerate(blocks_of(n)):
                    u = UNITS_BEFORE[n] + x
                    if u == 0:
                        pe.wait_ge(q["lv_lo_made"], per_pair(g, pair, 4, 4))
                    elif u >= 2:
                        pe.wait_ge(q["pt_lo_made"], per_pair(g, pair, T_UNITS, u - 1))
                    for b in range(b0, b1):
                        mm = pe.transpose(ps[:, 4 + u % 2, P * (b - b0):P * (b - b0) + P],
                                          probs[:, n % P_BUFS, P * b:P * b + P], ident[:])
                    mm.then_inc(q["turned"], 1)

            def with_values(g, pair, m):
                step, c = divmod(m, ST // 2)
                a, latent = divmod(step, 2)
                pe.wait_ge(q["pt_lo_made"], per_pair(g, pair, T_UNITS, UNITS_BEFORE[2 * m + 2]))
                if m >= 2:
                    pe.wait_ge(q["o_lo_made"], per_pair(g, pair, CHUNKS, m - 1))
                vals = [w[:, a] for w in (lv_hi, lv_lo)] if latent else [v_hi[:], v_lo[:]]
                last = 2 * c + 1
                for j in range(last + 1):
                    q0 = P if j == last else 0
                    mm = three(ps[:, 6 + m % 2, q0:256], [w[:, j, :] for w in vals],
                               [w[:, m % 2, 256 * j + q0:256 * j + 256] for w in (pt_hi, pt_lo)], j == 0, j == last)
                mm.then_inc(q["pv_mm"], 1)

            def outputs(g, pair, t):
                if t == 0:
                    pe.wait_ge(q["w_lo_dve"], SEED + per_pair(g, pair, 2, 2))
                pe.wait_ge(q["o_lo_made"], per_pair(g, pair, CHUNKS, 3 * ST // 2 + t // 2 + 1))
                if t >= 4:
                    pe.wait_ge(q["out_added"], SEED + per_pair(g, pair, ST, t - 3))
                for step in range(STEPS):
                    a, latent = divmod(step, 2)
                    lhs = [w[:, a, P * t:P * t + P] for w in ((ql_hi, ql_lo) if latent else (o_hi, o_lo))]
                    mm = three(ps[:, t % 4, :], lhs, [w[:, step, :] for w in o_w], step == 0, step == STEPS - 1)
                mm.then_inc(q["out_mm"], 1)

            pe.sem_inc(q["pv_mm"], SEED)
            pe.sem_inc(q["out_mm"], SEED)
            latent_query()
            pe.wait_ge(q["lq_lo_made"], 2)
            pe.wait_ge(q["const_made"], 6)
            with pe.Fori(0, GROUPS) as g:
                for pair in range(PAIRS):
                    for u in range(len(UNITS[pair]) + 2):
                        if u < len(UNITS[pair]):
                            unit(g, pair, u)
                        if 0 <= u - 2 < ROPES[pair]:
                            turn_roped(g, pair, u - 2)
                    for k in range(TILES + T_LAG + 2):
                        if k < TILES:
                            scores(g, pair, k)
                        if 0 <= k - T_LAG < TILES:
                            turn_probs(g, pair, k - T_LAG)
                        m = k - 2 - T_LAG
                        if m >= 0 and m % 2 == 0:
                            with_values(g, pair, m // 2)
                    for t in range(ST):
                        outputs(g, pair, t)

            ra = raw[:, 0, 0:CT * (E + E * R)].rearrange("p (c n) -> p c n", c=CT)
            for t in range(ST + 2):
                if t < ST:
                    pe.wait_ge(q["x1_made"], t + 1)
                    if t >= 2:
                        pe.wait_ge(q["x1T_made"], t - 1)
                    for c in range(CT):
                        mm = pe.transpose(ps[:, t % 2, P * c:P * c + P], acc[:, t, P * c:P * c + P], ident[:])
                    mm.then_inc(q["x1_turned"], 1)
                if t >= 2:
                    if t == 2:
                        pe.wait_ge(q["ffn_in"], 32)
                        pe.wait_ge(q["out_added"], SEED + GROUPS * PAIRS * ST)
                    pe.wait_ge(q["x1T_made"], t - 1)
                    for c in range(CT):
                        mm = pe.matmul(ps[:, 4 + (t - 2) // 2, 256 * (t % 2):256 * (t % 2) + E + E * R],
                                       probs[:].rearrange("p b n -> p (b n)")[:, 512 * ((t - 2) % 6) + P * c:512 * ((t - 2) % 6) + P * c + P],
                                       ra[:, c, :], start=c == 0 and t % 2 == 0, stop=c == CT - 1 and t % 2 == 1,
                                       skip_group_check=True)
                    mm.then_inc(q["logits_mm"], 1)
            for t in range(ST + 1):
                if t < ST:
                    pe.wait_ge(q["wh_made"], t + 1)
                    if t >= 2:
                        pe.wait_ge(q["whT_made"], t - 1)
                    pe.transpose(ps[:, t % 2, 0:P], raw[:, 2, P * t:P * t + P], ident[:]).then_inc(q["wh_turned"], 1)
                if t >= 1:
                    pe.wait_ge(q["whT_made"], t)
                    if t >= 3:
                        pe.wait_ge(q["y_added"], t - 2)
                    pe.matmul(ps[:, 2 + (t - 1) % 2, :], probs[:, 0, P * ((t - 1) % 2):P * ((t - 1) % 2) + P],
                              raw[:, 1, 0:D], start=True, stop=True).then_inc(q["y_mm"], 1)

        @block.scalar
        def _(act):
            def hi(dst, src):
                return nc.scalar.activation(dst, src, ACT.Copy)

            def weights_hi(g, name):
                load_landed(act, g, name)
                hi(parts(name)[0], raw_of(name)).then_inc(q["w_hi"], 1)

            xraw = acc[:].rearrange("p t n -> p (t n)").rearrange("p (c n) -> p c n", c=CT)
            act.wait_ge(q["wlq_in"], 16)
            hi(pt_hi[:, 0, 0:512], probs[:, 0, 0:512]).then_inc(q["wlq_hi_made"], 1)
            act.wait_ge(q["x_in"], 16)
            for c in range(CT):
                hi(x_hi[:, c, :], xraw[:, c, :]).then_inc(q["x_hi_made"], 1)
            for n in range(2):
                act.wait_ge(q["lq_mm"], n + 1)
                hi(lq_hi[:, 512 * n:512 * n + 512], ps[:, 4 + n, :]).then_inc(q["lq_hi_made"], 1)

            with act.Fori(0, GROUPS) as g:
                for pair in range(PAIRS):
                    act.wait_ge(q["pv_mm"], SEED + per_pair(g, pair, CHUNKS, 0))
                    act.wait_ge(q["wlk_in"], g * 32 + 16 * (pair + 1))
                    weights_hi(g, f"q{pair}")
                    hi(wlk_hi[:], wlk_raw[:]).then_inc(q["wlk_hi_made"], 1)
                    if pair == 0:
                        weights_hi(g, "kv")
                    act.wait_ge(q["out_mm"], SEED + per_pair(g, pair, ST, 0))
                    weights_hi(g, f"lv{pair}")

                    for u in range(len(UNITS[pair]) + 2):
                        if u < len(UNITS[pair]):
                            kind, t = UNITS[pair][u]
                            bank = 4 + u % BANKS
                            if kind == "kv":
                                act.wait_ge(q["rope_mul"], rope_base(g, pair, u + 1))
                                hi(v_hi[:, t, :], ps[:, bank, P:2 * P]).then_inc(q["v_hi_made"], 1)
                            if kind == "lv":
                                act.wait_ge(q["lv_mm"], per_pair(g, pair, 4, t + 1))
                                hi(lv_hi[:, :, 2 * t:2 * t + 2, :].rearrange("p a t d -> p t a d"),
                                   ps[:, bank, :].rearrange("p (t a d) -> p t a d", t=2, a=2)).then_inc(q["lv_hi_made"], 1)
                        r = u - 2
                        if 0 <= r < ROPES[pair]:
                            kind, t = UNITS[pair][r]
                            act.wait_ge(q["rope_t"], rope_base(g, pair, r + 1))
                            if kind == "ql":
                                hi(ql_hi[:, :, P * t:P * t + P],
                                   ps[:, r % 2, :].rearrange("p (a n) -> p a n", a=4)).then_inc(q["rope_hi"], 1)
                            else:
                                hi(k_hi[:, P * t:P * t + P], ps[:, r % 2, 0:P]).then_inc(q["rope_hi"], 1)

                    for k in range(TILES + T_LAG + 2):
                        m = k - 3 - T_LAG
                        if m >= 0 and m % 2 == 0:
                            m //= 2
                            step, c = divmod(m, ST // 2)
                            a, latent = divmod(step, 2)
                            act.wait_ge(q["pv_mm"], SEED + per_pair(g, pair, CHUNKS, m + 1))
                            hi((ql_hi if latent else o_hi)[:, a, 256 * c:256 * c + 256],
                               ps[:, 6 + m % 2, 0:256]).then_inc(q["o_hi_made"], 1)
                            if m == CHUNKS - 2:
                                weights_hi(g, f"oa{pair}")
                                weights_hi(g, f"ob{pair}")
                        n = k - T_LAG
                        if 0 <= n < TILES:
                            for x, (b0, b1) in enumerate(blocks_of(n)):
                                u = UNITS_BEFORE[n] + x
                                act.wait_ge(q["turned"], per_pair(g, pair, T_UNITS, u + 1))
                                half = pt_hi[:, (n // 2) % 2, :].rearrange("p (j n) -> p j n", j=ST)
                                hi(half[:, b0:b1, P * (n % 2):P * (n % 2) + P],
                                   ps[:, 4 + u % 2, 0:P * (b1 - b0)].rearrange("p (j n) -> p j n", n=P)
                                   ).then_inc(q["pt_hi_made"], 1)
                        if k < TILES:
                            i = k % ST
                            at, end = pieces_of(i)[0][0], pieces_of(i)[-1][0] + pieces_of(i)[-1][1]
                            bank = ps[:, 2 * (k % 2):2 * (k % 2) + 2, :].rearrange("p b n -> p (b n)")
                            act.wait_ge(q["maxed"], per_pair(g, pair, TILES, k + 1))
                            if k >= P_BUFS:
                                act.wait_ge(q["turned"], per_pair(g, pair, T_UNITS, UNITS_BEFORE[k - P_BUFS + 1]))
                            nc.scalar.activation(probs[:, k % P_BUFS, 0:P * (i + 1)], bank[:, at:end], ACT.Exp,
                                                 bias=neg_max[:, k % 4:k % 4 + 1], scale=1.0,
                                                 accum_out=row_sum[:, k % 4:k % 4 + 1]).then_inc(q["exped"], 1)

            def roots(signal, made):
                for half in range(2):
                    ts = slice(LN_TILES * half, LN_TILES * (half + 1))
                    act.wait_ge(q[signal], half + 1)
                    nc.scalar.activation(root[:, ts], ve[:, ts], ACT.Sqrt).then_inc(q[made], 1)

            roots("ve_made", "root_made")
            for t in range(ST):
                act.wait_ge(q["x1_turned"], t + 1)
                if t >= 6:
                    act.wait_ge(q["logits_mm"], t - 5)
                nc.scalar.activation(probs[:].rearrange("p b n -> p (b n)")[:, 512 * (t % 6):512 * (t % 6) + 512],
                                     ps[:, t % 2, :], ACT.Copy).then_inc(q["x1T_made"], 1)
            act.wait_ge(q["logits_mm"], ST)
            for t in range(ST):
                act.wait_ge(q["wh_turned"], t + 1)
                if t >= 2:
                    act.wait_ge(q["y_mm"], t - 1)
                nc.scalar.activation(probs[:, 0, P * (t % 2):P * (t % 2) + P], ps[:, t % 2, 0:P],
                                     ACT.Copy).then_inc(q["whT_made"], 1)
            roots("ve2_made", "root2_made")

        @block.gpsimd
        def _(pool):
            pool.sem_inc(q["w_lo_pool"], SEED)
            pool.sem_inc(q["wlk_lo_made"], SEED)
            chain = [0]

            def link(ins):
                chain[0] += 1
                ins.then_inc(q["const_made"], 1)
                pool.wait_ge(q["const_made"], chain[0])

            link(nc.gpsimd.memset(ident[:], 0.0))
            link(nc.gpsimd.affine_select(out=ident[:], in_=ident[:], compare_op=ALU.not_equal, fill=1.0, base=0,
                                         pattern=[[-1, P]], channel_multiplier=1))
            link(nc.gpsimd.tensor_copy(ident_b[:], ident[:]))
            link(nc.gpsimd.memset(mask_b[:], 0.0))
            link(nc.gpsimd.affine_select(out=mask_b[:], in_=mask_b[:], compare_op=ALU.is_ge, fill=MASKED, base=0,
                                         pattern=[[-1, P]], channel_multiplier=1))
            link(nc.gpsimd.iota(order[:], pattern=[[-1, E]], base=E, channel_multiplier=0,
                                allow_small_or_imprecise_dtypes=True))

            def weights_lo(g, name):
                pool.wait_ge(q["w_hi"], g * len(LOADS) + (LOADS.index(name) + 1))
                h, l = parts(name)
                nc.gpsimd.tensor_tensor(l, raw_of(name), h, ALU.subtract).then_inc(q["w_lo_pool"], 1)

            with pool.Fori(0, GROUPS) as g:
                for pair in range(PAIRS):
                    weights_lo(g, f"q{pair}")
                    pool.wait_ge(q["wlk_hi_made"], per_pair(g, pair, 1, 1))
                    nc.gpsimd.tensor_tensor(wlk_lo[:], wlk_raw[:], wlk_hi[:], ALU.subtract).then_inc(q["wlk_lo_made"], 1)
                    if pair == 0:
                        weights_lo(g, "kv")
                    weights_lo(g, f"lv{pair}")
                    for r in range(ROPES[pair]):
                        n = 4 * P if UNITS[pair][r][0] == "ql" else P
                        b = probs[:, r % P_BUFS, :]
                        pool.wait_ge(q["rope_mul"], rope_base(g, pair, r + 1))
                        nc.gpsimd.tensor_tensor(b[:, 0:n], b[:, 0:n], b[:, 512:512 + n], ALU.add).then_inc(q["rope_add"], 1)
                    for k in range(TILES):
                        w = P * (k % ST + 1)
                        b = probs[:, k % P_BUFS, 0:w]
                        pool.wait_ge(q["inverted"], per_pair(g, pair, TILES, k + 1))
                        nc.gpsimd.tensor_tensor(b, b, inv_sum[:, k % 4:k % 4 + 1].to_broadcast([P, w]),
                                                ALU.mult).then_inc(q["normed"], 1)

        @block.vector
        def _(dve):
            def lo(dst, src, h):
                return nc.vector.tensor_tensor(dst, src, h, ALU.subtract)

            dve.sem_inc(q["w_lo_dve"], SEED)
            dve.sem_inc(q["out_added"], SEED)
            xraw = acc[:].rearrange("p t n -> p (t n)").rearrange("p (c n) -> p c n", c=CT)
            dve.wait_ge(q["wlq_hi_made"], 1)
            lo(pt_lo[:, 0, 0:512], probs[:, 0, 0:512], pt_hi[:, 0, 0:512]).then_inc(q["wlq_lo_made"], 1)
            for c in range(CT):
                dve.wait_ge(q["x_hi_made"], c + 1)
                lo(x_lo[:, c, :], xraw[:, c, :], x_hi[:, c, :]).then_inc(q["x_lo_made"], 1)
            for n in range(2):
                dve.wait_ge(q["lq_hi_made"], n + 1)
                lo(lq_lo[:, 512 * n:512 * n + 512], ps[:, 4 + n, :], lq_hi[:, 512 * n:512 * n + 512]
                   ).then_inc(q["lq_lo_made"], 1)
            dve.wait_ge(q["tab_in"], 32)
            dve.wait_ge(q["res_in"], 16)

            def rope(g, pair, r):
                kind, t = UNITS[pair][r]
                if kind == "ql":
                    n = sum(k == "ql" for k, _ in UNITS[pair][:r + 1])
                    dve.wait_ge(q["ql_mm"], per_pair(g, pair, ST, n))
                else:
                    dve.wait_ge(q["kv_mm"], g * ST + (t + 1))
                h = 4 if kind == "ql" else 1
                src = ps[:, 4 + r % BANKS, 0:P * h].rearrange("p (h f d) -> p h f d", h=h, f=2)
                b = probs[:, r % P_BUFS, :]
                with_cos = b[:, 0:P * h].rearrange("p (h f d) -> p (h f) d", h=h, f=2)
                with_sin = b[:, 512:512 + P * h].rearrange("p (h f d) -> p h f d", h=h, f=2)
                c_t, s_t = cos_sb[:, t:t + 1, :], sin_sb[:, t:t + 1, :]
                nc.vector.tensor_tensor(with_cos, src.rearrange("p h f d -> p (h f) d"),
                                        c_t.to_broadcast([P, 2 * h, HALF]), ALU.mult)
                nc.vector.scalar_tensor_tensor(out=with_sin[:, :, 0, :], in0=src[:, :, 1, :], scalar=-1.0,
                                               in1=s_t.to_broadcast([P, h, HALF]), op0=ALU.mult, op1=ALU.mult)
                nc.vector.tensor_tensor(with_sin[:, :, 1, :], src[:, :, 0, :],
                                        s_t.to_broadcast([P, h, HALF]), ALU.mult).then_inc(q["rope_mul"], 1)

            with dve.Fori(0, GROUPS) as g:
                for pair in range(PAIRS):
                    for u in range(len(UNITS[pair]) + 3):
                        if u < ROPES[pair]:
                            rope(g, pair, u)
                        if 0 <= u - 1 < len(UNITS[pair]):
                            kind, t = UNITS[pair][u - 1]
                            bank = 4 + (u - 1) % BANKS
                            if kind == "kv":
                                dve.wait_ge(q["v_hi_made"], g * ST + (t + 1))
                                lo(v_lo[:, t, :], ps[:, bank, P:2 * P], v_hi[:, t, :]).then_inc(q["v_lo_made"], 1)
                            if kind == "lv":
                                dve.wait_ge(q["lv_hi_made"], per_pair(g, pair, 4, t + 1))
                                lo(lv_lo[:, :, 2 * t:2 * t + 2, :].rearrange("p a t d -> p t a d"),
                                   ps[:, bank, :].rearrange("p (t a d) -> p t a d", t=2, a=2),
                                   lv_hi[:, :, 2 * t:2 * t + 2, :].rearrange("p a t d -> p t a d")
                                   ).then_inc(q["lv_lo_made"], 1)
                        r = u - 3
                        if 0 <= r < ROPES[pair]:
                            kind, t = UNITS[pair][r]
                            dve.wait_ge(q["rope_hi"], rope_base(g, pair, r + 1))
                            if kind == "ql":
                                lo(ql_lo[:, :, P * t:P * t + P], ps[:, r % 2, :].rearrange("p (a n) -> p a n", a=4),
                                   ql_hi[:, :, P * t:P * t + P]).then_inc(q["rope_lo"], 1)
                            else:
                                lo(k_lo[:, P * t:P * t + P], ps[:, r % 2, 0:P], k_hi[:, P * t:P * t + P]
                                   ).then_inc(q["rope_lo"], 1)

                    for k in range(TILES + T_LAG + 2):
                        n = k - 1 - T_LAG
                        if 0 <= n < TILES:
                            for x, (b0, b1) in enumerate(blocks_of(n)):
                                u = UNITS_BEFORE[n] + x
                                dve.wait_ge(q["pt_hi_made"], per_pair(g, pair, T_UNITS, u + 1))
                                h, l = (w[:, (n // 2) % 2, :].rearrange("p (j n) -> p j n", j=ST)
                                        [:, b0:b1, P * (n % 2):P * (n % 2) + P] for w in (pt_hi, pt_lo))
                                lo(l, ps[:, 4 + u % 2, 0:P * (b1 - b0)].rearrange("p (j n) -> p j n", n=P), h
                                   ).then_inc(q["pt_lo_made"], 1)
                        if n == TILES - 1:
                            for name in (f"oa{pair}", f"ob{pair}"):
                                dve.wait_ge(q["w_hi"], g * len(LOADS) + (LOADS.index(name) + 1))
                                lo(parts(name)[1], raw_of(name), parts(name)[0]).then_inc(q["w_lo_dve"], 1)
                        if k < TILES:
                            i = k % ST
                            at, end = pieces_of(i)[0][0], pieces_of(i)[-1][0] + pieces_of(i)[-1][1]
                            bank = ps[:, 2 * (k % 2):2 * (k % 2) + 2, :].rearrange("p b n -> p (b n)")
                            dve.wait_ge(q["scored"], per_pair(g, pair, TILES, k + 1))
                            nc.vector.tensor_reduce(neg_max[:, k % 4:k % 4 + 1], bank[:, at:end], AX.X, ALU.max,
                                                    negate=True).then_inc(q["maxed"], 1)
                        if 0 <= k - 1 < TILES:
                            n = (k - 1) % 4
                            dve.wait_ge(q["exped"], per_pair(g, pair, TILES, k))
                            nc.vector.reciprocal(inv_sum[:, n:n + 1], row_sum[:, n:n + 1]).then_inc(q["inverted"], 1)
                        m = k - 3 - T_LAG
                        if m >= 0 and m % 2 == 0:
                            m //= 2
                            step, c = divmod(m, ST // 2)
                            a, latent = divmod(step, 2)
                            h, l = (w[:, a, 256 * c:256 * c + 256] for w in ((ql_hi, ql_lo) if latent else (o_hi, o_lo)))
                            dve.wait_ge(q["o_hi_made"], per_pair(g, pair, CHUNKS, m + 1))
                            lo(l, ps[:, 6 + m % 2, 0:256], h).then_inc(q["o_lo_made"], 1)

                    for t in range(ST):
                        dve.wait_ge(q["out_mm"], SEED + per_pair(g, pair, ST, t + 1))
                        nc.vector.tensor_tensor(acc[:, t, :], ps[:, t % 4, :], acc[:, t, :], ALU.add
                                                ).then_inc(q["out_added"], 1)

            def link(name, count, ins):
                count[0] += 1
                ins.then_inc(q[name], 1)
                dve.wait_ge(q[name], count[0])

            def moments(name, count, t):
                link(name, count, nc.vector.bn_stats(stats[:, t, 0:6], acc[:, t, :]))
                link(name, count, nc.vector.bn_aggr(stats[:, t, 6:8], stats[:, t, 0:6]))

            def var_eps(half, signal):
                ts = slice(LN_TILES * half, LN_TILES * (half + 1))
                nc.vector.tensor_scalar(ve[:, ts], stats[:, ts, 7], EPS, None, ALU.add).then_inc(q[signal], 1)

            def inverse_root(name, count, half, signal):
                ts = slice(LN_TILES * half, LN_TILES * (half + 1))
                dve.wait_ge(q[signal], half + 1)
                link(name, count, nc.vector.reciprocal(rstd[:, ts], root[:, ts]))
                link(name, count, nc.vector.tensor_tensor(newton[:, ts], rstd[:, ts], rstd[:, ts], ALU.mult))
                link(name, count, nc.vector.tensor_tensor(newton[:, ts], newton[:, ts], ve[:, ts], ALU.mult))
                link(name, count, nc.vector.tensor_scalar(newton[:, ts], newton[:, ts], -0.5, 1.5, ALU.mult, ALU.add))
                link(name, count, nc.vector.tensor_tensor(rstd[:, ts], rstd[:, ts], newton[:, ts], ALU.mult))

            def finish(count, half):
                inverse_root("ln2_chain", count, half, "root2_made")
                for t in range(LN_TILES * half, LN_TILES * (half + 1)):
                    normalize(t).then_inc(q["finished"], 1)

            def normalize(t):
                return nc.vector.tensor_scalar(acc[:, t, :], acc[:, t, :], stats[:, t, 6:7], rstd[:, t:t + 1],
                                               ALU.subtract, ALU.mult)

            dve.wait_ge(q["out_added"], SEED + GROUPS * PAIRS * ST)
            ln = [0]
            for half in range(2):
                for t in range(LN_TILES * half, LN_TILES * (half + 1)):
                    moments("ln_chain", ln, t)
                var_eps(half, "ve_made")
            for half in range(2):
                inverse_root("ln_chain", ln, half, "root_made")
                for t in range(LN_TILES * half, LN_TILES * (half + 1)):
                    normalize(t).then_inc(q["x1_made"], 1)

            def step(ins):
                chain[0] += 1
                ins.then_inc(q["route_chain"], 1)
                dve.wait_ge(q["route_chain"], chain[0])

            chain = [0]
            dve.wait_ge(q["logits_mm"], ST)
            mix = ps[:, 4:8, :].rearrange("p b (y n) -> p (b y) n", y=2)
            logits, equal, ranked, first, weight = (route[:, i] for i in range(5))
            step(nc.vector.tensor_copy(logits, mix[:, :, 0:E]))
            step(nc.vector.tensor_reduce(top[:], logits, AX.X, ALU.max))
            step(nc.vector.tensor_tensor(equal, logits, top[:, :, None].to_broadcast([P, ST, E]), ALU.is_equal))
            step(nc.vector.tensor_tensor(ranked, equal, order[:, None, :].to_broadcast([P, ST, E]), ALU.mult))
            step(nc.vector.tensor_reduce(top2[:], ranked, AX.X, ALU.max))
            step(nc.vector.tensor_tensor(first, ranked, top2[:, :, None].to_broadcast([P, ST, E]), ALU.is_equal))
            step(nc.vector.tensor_tensor(weight, first, top[:, :, None].to_broadcast([P, ST, E]), ALU.mult))
            for t in range(ST):
                nc.vector.tensor_tensor(raw[:, 2, P * t:P * t + P].rearrange("p (e r) -> p e r", e=E),
                                        mix[:, t, E:E + E * R].rearrange("p (e r) -> p e r", e=E),
                                        weight[:, t, :, None].to_broadcast([P, E, R]), ALU.mult).then_inc(q["wh_made"], 1)
            ln2 = [0]
            for half in range(2):
                for t in range(LN_TILES * half, LN_TILES * (half + 1)):
                    dve.wait_ge(q["y_mm"], t + 1)
                    nc.vector.tensor_tensor(acc[:, t, :], ps[:, 2 + t % 2, :], acc[:, t, :], ALU.add
                                            ).then_inc(q["y_added"], 1)
                    dve.wait_ge(q["y_added"], t + 1)
                    moments("ln2_chain", ln2, t)
                var_eps(half, "ve2_made")
                if half == 1:
                    finish(ln2, 0)
            finish(ln2, 1)


def rope_tables():
    inv_freq = (np.float32(1.0) / np.float32(10000.0) ** (np.arange(0, HD, 2, dtype=np.float32) / np.float32(HD)))
    angle = np.outer(np.arange(S, dtype=np.float32), inv_freq.astype(np.float32)).astype(np.float32)
    share = float(HD) ** -0.25
    tables = [(f(angle.astype(np.float64)) * share).astype(np.float32) for f in (np.cos, np.sin)]
    return [np.ascontiguousarray(t.reshape(ST, P, HALF).transpose(1, 0, 2)) for t in tables]


def kernel(**inputs):
    import concourse.bacc as bacc
    from concourse.bass_utils import run_bass_kernel_spmd

    a = {k.replace("L0_attn_", "").replace("L0_ffn_", ""): np.asarray(v) for k, v in inputs.items()}
    x = a["hidden_states"][0]

    def by_pair(w):
        return w.reshape(CT, P, GROUPS, PAIRS, 256).transpose(2, 3, 1, 0, 4).reshape(GROUPS, PAIRS, P, CT * 256)

    cos, sin = rope_tables()
    kv = np.stack([a[n].reshape(CT, P, GROUPS, HD) for n in ("w_k", "w_v")], axis=3)
    wo = np.stack([a[n].reshape(GROUPS, PAIRS, 2, HD, D) for n in ("w_o", "w_lo")], axis=4)
    arrays = {
        "xT": x.T.reshape(CT, P, S).transpose(1, 0, 2).reshape(P, CT * S),
        "x": x.reshape(ST, P, D).transpose(1, 0, 2),
        "wlq": a["w_lq"].reshape(CT, P, P).transpose(1, 0, 2).reshape(P, CT * P),
        "wq": by_pair(a["w_q"]),
        "wkv": kv.transpose(2, 1, 0, 3, 4).reshape(GROUPS, P, CT * 256),
        "wlk": a["w_lk"].reshape(P, GROUPS, PAIRS, 256).transpose(1, 2, 0, 3),
        "wlv": by_pair(a["w_lv"]),
        "wo": wo.transpose(0, 1, 2, 3, 4, 5).reshape(GROUPS, PAIRS, 2, P, 2 * D),
        "cos": cos,
        "sin": sin,
        "route_a": np.concatenate([a["route_w"], a["A"].reshape(E * R, D)]).T.reshape(CT, P, E + E * R)
                     .transpose(1, 0, 2).reshape(P, CT * (E + E * R)),
        "bwT": a["Bw"].transpose(0, 2, 1).reshape(E * R, D),
    }
    arrays = {k: np.ascontiguousarray(v) for k, v in arrays.items()}
    nc = bacc.Bacc("TRN2", target_bir_lowering=False, num_devices=1)
    args = [nc.dram_tensor(k, v.shape, F32, kind="ExternalInput").ap() for k, v in arrays.items()]
    out = nc.dram_tensor("out", (S, D), F32, kind="ExternalOutput").ap()
    block_kernel(nc, *args, out.rearrange("(t p) n -> p t n", p=P))
    r = run_bass_kernel_spmd(nc, [arrays], core_ids=[0])
    return r.results[0]["out"].reshape(1, S, D)
```

```python
from contextlib import ExitStack

import numpy as np

import concourse.bass as bass
from concourse import mybir

P = 128
F32 = mybir.dt.float32
F32R = mybir.dt.float32r
BF16 = mybir.dt.bfloat16
ALU = mybir.AluOpType
ACT = mybir.ActivationFunctionType
AX = mybir.AxisListType

S, D = 1024, 512
H, KVH, HD = 32, 8, 128
E, R = 8, 16
GROUPS = KVH
PAIRS = 2
CT = D // P
ST = S // P
HALF = HD // 2
EPS = 1e-5
MASKED = -1e30

STEPS = 4
TILES = STEPS * ST
CHUNKS = TILES // 2
LONG_BANKS = ((0, 1),)
SHORT_BANK = 2
T_BANKS = (3, 4, 5)
O_BANKS = (6, 7)
O_LAG_LONG = 3
PV_SHORT = 3
PV_SPLIT = True
PV_SHORT_BEFORE = False
ACT_ORDER = 'hoe'
DVE_ORDER = 'lmro'
HL = 0
LL = 1
OL = 0
R_LAG = 3
EARLY = 2
EARLY_E = 2
T_LAG = 3
P_BUFS = 4
RAW_SLOTS = 3
SEED = 1
RAW_COLS = 1024

LOADS = ("q0", "kv", "lv0", "oa0", "ob0", "q1", "lv1", "oa1", "ob1")
POOL_LO = ("q0", "kv", "lv0", "q1", "lv1")
OUT_PARTS = (("ob", 0, 512, 1536), ("oa", 0, 1024, 0), ("ob", 512, 512, 1024))
OUT_AFTER = (CHUNKS - 4, CHUNKS - 3, CHUNKS - 1)
STEP_WEIGHTS = ((2, 0), (2, 512), (2, 1536), (3, 1024))

UNITS = (
    [x for t in range(ST) for x in (("ql", t), ("kv", t))] + [("lv", x) for x in range(ST // 2)],
    [("ql", t) for t in range(ST)] + [("lv", x) for x in range(ST // 2)],
)
ROPES = tuple(sum(k != "lv" for k, _ in u) for u in UNITS)
LN_TILES = ST // 2
ORDER = (4, 3, 5, 2, 6, 1, 7, 0)
OUT_ORDER = tuple(2 * (ORDER[n] // 2) + x for n in (2, 3, 6, 7) for x in range(2))
BANKS = 4


def chunk_after(n):
    return n // 4 * 2 + n % 2, n // ST, ORDER[n % ST] // 2


PV_BEFORE, PV_AFTER, O_SLOT = {}, {}, {}
for _n in range(TILES):
    if _n % 4 == 2 and not PV_SPLIT:
        PV_AFTER.setdefault(_n + 1 + T_LAG, []).append((_n, 0, 2 * (ORDER[_n % ST] // 2) + 2))
        O_SLOT[_n + O_LAG_LONG + T_LAG] = _n
    elif _n % 4 == 2:
        _blocks = 2 * (ORDER[_n % ST] // 2) + 2
        PV_AFTER.setdefault(_n + 1 + T_LAG, []).append((_n, 0, _blocks // 2))
        PV_BEFORE.setdefault(_n + 2 + T_LAG, []).append((_n, _blocks // 2, _blocks))
        O_SLOT[_n + O_LAG_LONG + T_LAG] = _n
    if _n % 4 == 3:
        (PV_BEFORE if PV_SHORT_BEFORE else PV_AFTER).setdefault(_n + PV_SHORT + T_LAG, []).append((_n, 0, 2 * (ORDER[_n % ST] // 2) + 2))
        O_SLOT[_n + PV_SHORT + 1 + T_LAG] = _n
SLOTS = TILES + T_LAG + PV_SHORT + 2


def turned_at(pair, u):
    last = ROPES[pair] + 1
    if R_LAG == 3 and u == last:
        return (u - 3, u - 2)
    return (u - R_LAG,) if R_LAG <= u <= last else ()


def part_of_pt(n):
    i = ORDER[n % ST]
    return n % 2, 4 if i < 2 else 0, P * (i % 2)


def blocks_of(n):
    i = ORDER[n % ST]
    return [(0, min(i, 3) + 1)] + ([(4, i + 1)] if i > 3 else [])


UNITS_BEFORE = [sum(len(blocks_of(t)) for t in range(n)) for n in range(TILES + 1)]
T_UNITS = UNITS_BEFORE[-1]


SCORE_BANKS = [(SHORT_BANK,) if n % 2 else LONG_BANKS[n // 2 % len(LONG_BANKS)] for n in range(TILES)]


def last_user(n, bank):
    return max((t for t in range(n) if bank in SCORE_BANKS[t]), default=None)


def block_kernel(nc, xT, x, wlq, wq, wkv, wlk, wlv, wo, cos, sin, route_a, bwT, out):
    with ExitStack() as ctx:
        def sb(name, shape, dt=F32):
            return ctx.enter_context(nc.sbuf_tensor(name, shape, dt))

        def sem(name):
            return ctx.enter_context(nc.semaphore(name))

        ps = ctx.enter_context(nc.psum_tensor("ps", [P, 8, 512], F32))

        x_hi, x_lo = sb("x_hi", [P, CT, S], F32R), sb("x_lo", [P, CT, S], F32R)
        lq_hi, lq_lo = sb("lq_hi", [P, S], F32R), sb("lq_lo", [P, S], F32R)
        k_hi, k_lo = sb("k_hi", [P, S], F32R), sb("k_lo", [P, S], F32R)
        v_hi, v_lo = sb("v_hi", [P, ST, HD], F32R), sb("v_lo", [P, ST, HD], F32R)
        ql_hi, ql_lo = sb("ql_hi", [P, 4, S], F32R), sb("ql_lo", [P, 4, S], F32R)
        lv_hi, lv_lo = sb("lv_hi", [P, 2, ST, HD], F32R), sb("lv_lo", [P, 2, ST, HD], F32R)
        o_hi, o_lo = sb("o_hi", [P, 2, S], F32R), sb("o_lo", [P, 2, S], F32R)
        pt_hi, pt_lo = sb("pt_hi", [P, 2, ST * 256], F32R), sb("pt_lo", [P, 2, ST * 256], F32R)
        wlk_raw = sb("wlk_raw", [P, 256])
        wlk_hi, wlk_lo = sb("wlk_hi", [P, 256], F32R), sb("wlk_lo", [P, 256], F32R)
        raw = sb("raw", [P, RAW_SLOTS, RAW_COLS])
        probs = sb("probs", [P, P_BUFS, S])
        acc = sb("acc", [P, ST, D])
        cos_sb, sin_sb = sb("cos_sb", [P, ST, HALF]), sb("sin_sb", [P, ST, HALF])
        ident = sb("ident", [P, P])
        ident_b, mask_b = sb("ident_b", [P, P], BF16), sb("mask_b", [P, P], BF16)
        neg_max, row_sum, inv_sum = sb("neg_max", [P, 4]), sb("row_sum", [P, 4]), sb("inv_sum", [P, 4])
        stats = sb("stats", [P, ST, 8])
        rstd, ve, root, newton = (sb(n, [P, ST]) for n in ("rstd", "ve", "root", "newton"))
        order = sb("order", [P, E])
        route = sb("route", [P, 5, ST, E])
        top = sb("top", [P, ST])
        top2 = sb("top2", [P, ST])

        def parts(name):
            half, at, n = {"q": (0, 0, 1024), "kv": (0, 1024, 1024), "lv": (1, 0, 1024)}[name.rstrip("01")]
            return pt_hi[:, half, at:at + n], pt_lo[:, half, at:at + n]

        q_w = [p.rearrange("p (c n) -> p c n", c=CT) for p in parts("q")]
        kv_w = [p.rearrange("p (c n) -> p c n", c=CT) for p in parts("kv")]
        lv_w = [p.rearrange("p (c n) -> p c n", c=CT) for p in parts("lv")]

        names = """x_in tab_in wlq_in res_in wlk_in ffn_in const_made x_hi_made x_lo_made wlq_hi_made wlq_lo_made
            lq_mm lq_hi_made lq_lo_made w_hi w_lo_pool wo_hi wo_lo wlk_hi_made wlk_lo_made
            ql_mm kv_mm lv_mm v_hi_made v_lo_made lv_hi_made lv_lo_made
            rope_mul rope_add rope_t rope_hi rope_lo
            scored maxed exped inverted normed turned pt_hi_made pt_lo_made pv_mm o_hi_made o_lo_made
            out_mm out_added ln_chain x1_made x1_turned x1T_made logits_mm route_chain wh_made wh_turned whT_made
            y_mm y_added ln2_chain ve_made root_made ve2_made root2_made finished stored""".split()
        q = {n: sem(n) for n in names}
        raw_in = [sem(f"raw_in{i}") for i in range(RAW_SLOTS)]

        def per_pair(g, pair, n, k):
            return g * (PAIRS * n) + (pair * n + k)

        def rope_base(g, pair, k):
            return g * sum(ROPES) + (pair * ROPES[0] + k)

        def load_landed(eng, g, name):
            i = LOADS.index(name)
            per_slot = len(LOADS) // RAW_SLOTS
            eng.wait_ge(raw_in[i % RAW_SLOTS], g * (16 * per_slot) + 16 * (i // RAW_SLOTS + 1))

        def output_weights(part, pair):
            name, at, n, to = OUT_PARTS[part]
            return (raw_of(f"{name}{pair}")[:, at:at + n], pt_hi[:, 1, to:to + n], pt_lo[:, 1, to:to + n])

        def raw_of(name):
            return raw[:, LOADS.index(name) % RAW_SLOTS, :]

        def scores_of(n):
            banks, w = SCORE_BANKS[n], P * (ORDER[n % ST] + 1)
            return ps[:, banks[0]:banks[-1] + 1:max(1, banks[-1] - banks[0]), 0:w // len(banks)]

        block = ctx.enter_context(nc.Block())

        @block.sync
        def _(sp):
            sp.dma_start(acc[:].rearrange("p t n -> p (t n)"), xT).then_inc(q["x_in"], 16)
            sp.dma_start(probs[:, 0, 0:512], wlq).then_inc(q["wlq_in"], 16)
            sp.dma_start(cos_sb[:], cos).then_inc(q["tab_in"], 16)
            sp.dma_start(sin_sb[:], sin).then_inc(q["tab_in"], 16)
            sp.wait_ge(q["x_lo_made"], CT)
            sp.dma_start(acc[:], x).then_inc(q["res_in"], 16)
            with sp.Fori(0, GROUPS) as g:
                for pair in range(PAIRS):
                    sp.wait_ge(q["wlk_lo_made"], SEED + per_pair(g, pair, 1, 0))
                    sp.dma_start(wlk_raw[:], wlk[g, pair]).then_inc(q["wlk_in"], 16)
                    for i, name in enumerate(LOADS):
                        if (i >= LOADS.index("q1")) != bool(pair):
                            continue
                        before = LOADS[i - RAW_SLOTS]
                        now = int(i >= RAW_SLOTS)
                        if before in POOL_LO:
                            n = POOL_LO.index(before) + 1
                            sp.wait_ge(q["w_lo_pool"], SEED + g * len(POOL_LO) + (n if now else 0))
                        else:
                            n = int(before[-1]) * 3 + (2 if before[:2] == "oa" else 3)
                            sp.wait_ge(q["wo_lo"], SEED + g * (PAIRS * 3) + (n if now else 0))
                        kind = name.rstrip("01")
                        src = {"q": lambda: wq[g, pair], "kv": lambda: wkv[g], "lv": lambda: wlv[g, pair],
                               "oa": lambda: wo[g, pair, 0], "ob": lambda: wo[g, pair, 1]}[kind]()
                        sp.dma_start(raw_of(name), src).then_inc(raw_in[i % RAW_SLOTS], 16)
            sp.wait_ge(q["wo_lo"], SEED + GROUPS * PAIRS * len(OUT_PARTS))
            sp.wait_ge(q["w_lo_pool"], SEED + GROUPS * len(POOL_LO))
            sp.dma_start(raw[:, 0, 0:CT * (E + E * R)], route_a).then_inc(q["ffn_in"], 16)
            sp.dma_start(raw[:, 1, 0:D], bwT).then_inc(q["ffn_in"], 16)
            for t in range(ST):
                sp.wait_ge(q["finished"], t + 1)
                sp.dma_start(out[:, t, :], acc[:, t, :]).then_inc(q["stored"], 16)
            sp.wait_ge(q["stored"], 16 * ST)

        @block.tensor
        def _(pe):
            def three(dst, hi_lo_a, hi_lo_b, first, last=False):
                (ah, al), (bh, bl) = hi_lo_a, hi_lo_b
                pe.matmul(dst, ah, bh, start=first, stop=False, skip_group_check=True)
                pe.matmul(dst, ah, bl, start=False, stop=False, skip_group_check=True)
                return pe.matmul(dst, al, bh, start=False, stop=last, skip_group_check=True)

            def x_tile(c, t):
                return [a[:, c, P * t:P * t + P] for a in (x_hi, x_lo)]

            def latent_query():
                pe.wait_ge(q["x_lo_made"], CT)
                pe.wait_ge(q["wlq_lo_made"], 1)
                for n in range(2):
                    for c in range(CT):
                        mm = three(ps[:, 4 + n, :],
                                   [a[:, 0, P * c:P * c + P] for a in (pt_hi, pt_lo)],
                                   [a[:, c, 512 * n:512 * n + 512] for a in (x_hi, x_lo)], c == 0, c == CT - 1)
                    mm.then_inc(q["lq_mm"], 1)

            def unit(g, pair, u):
                kind, t = UNITS[pair][u]
                bank = 4 + u % BANKS
                if u >= BANKS:
                    k0, t0 = UNITS[pair][u - BANKS]
                    if k0 == "ql":
                        n = sum(k != "lv" for k, _ in UNITS[pair][:u - BANKS + 1])
                        pe.wait_ge(q["rope_mul"], rope_base(g, pair, n))
                    elif k0 == "kv":
                        pe.wait_ge(q["v_lo_made"], g * ST + (t0 + 1))
                if kind == "ql":
                    if t == 0:
                        pe.wait_ge(q["w_lo_pool"], SEED + g * len(POOL_LO) + (POOL_LO.index(f"q{pair}") + 1))
                        pe.wait_ge(q["wlk_lo_made"], SEED + per_pair(g, pair, 1, 1))
                    for c in range(CT):
                        three(ps[:, bank, 0:256], x_tile(c, t), [w[:, c, :] for w in q_w], c == 0)
                    three(ps[:, bank, 256:512], [a[:, P * t:P * t + P] for a in (lq_hi, lq_lo)],
                          [wlk_hi[:], wlk_lo[:]], False, True).then_inc(q["ql_mm"], 1)
                elif kind == "kv":
                    if t == 0:
                        pe.wait_ge(q["w_lo_pool"], SEED + g * len(POOL_LO) + (POOL_LO.index("kv") + 1))
                    for c in range(CT):
                        mm = three(ps[:, bank, 0:256], x_tile(c, t), [w[:, c, :] for w in kv_w], c == 0, c == CT - 1)
                    mm.then_inc(q["kv_mm"], 1)
                else:
                    if t == 0:
                        pe.wait_ge(q["w_lo_pool"], SEED + g * len(POOL_LO) + (POOL_LO.index(f"lv{pair}") + 1))
                    for y in range(2):
                        for c in range(CT):
                            mm = three(ps[:, bank, 256 * y:256 * y + 256], x_tile(c, 2 * t + y),
                                       [w[:, c, :] for w in lv_w], c == 0 and y == 0, c == CT - 1 and y == 1)
                    mm.then_inc(q["lv_mm"], 1)

            def turn_roped(g, pair, r):
                pe.wait_ge(q["rope_add"], rope_base(g, pair, r + 1))
                if r == 0:
                    pe.wait_ge(q["out_added"], SEED + per_pair(g, pair, ST, 0))
                else:
                    if r >= 2:
                        pe.wait_ge(q["rope_lo"], rope_base(g, pair, r - 1))
                n = 4 if UNITS[pair][r][0] == "ql" else 1
                for b in range(n):
                    mm = pe.transpose(ps[:, r % 2, P * b:P * b + P], probs[:, r % P_BUFS, P * b:P * b + P], ident[:])
                mm.then_inc(q["rope_t"], 1)

            def scores(g, pair, n):
                i = ORDER[n % ST]
                a, latent = divmod(n // ST, 2)
                if n == 0:
                    pe.wait_ge(q["rope_lo"], rope_base(g, pair, ROPES[pair]))
                keys = (ql_hi[:, 2 + a, :], ql_lo[:, 2 + a, :]) if latent else (k_hi[:], k_lo[:])
                lhs = [w[:, a, P * i:P * i + P] for w in (ql_hi, ql_lo)]
                w = P * (i + 1) // len(SCORE_BANKS[n])
                for x, bank in enumerate(SCORE_BANKS[n]):
                    last = last_user(n, bank)
                    if last is not None:
                        pe.wait_ge(q["exped"], per_pair(g, pair, TILES, last + 1))
                    mm = three(ps[:, bank, 0:w], lhs, [t[:, w * x:w * x + w] for t in keys], True)
                pe.matmul(ps[:, bank, w - P:w], ident_b[:], mask_b[:], start=False, stop=True,
                          skip_group_check=True).then_inc(q["scored"], 1)

            def turn_probs(g, pair, n):
                pe.wait_ge(q["normed"], per_pair(g, pair, TILES, n + 1))
                if n == 0:
                    pe.wait_ge(q["lv_lo_made"], per_pair(g, pair, 4, 4))
                for x, (b0, b1) in enumerate(blocks_of(n)):
                    u = UNITS_BEFORE[n] + x
                    if u >= len(T_BANKS):
                        pe.wait_ge(q["pt_lo_made"], per_pair(g, pair, T_UNITS, u - len(T_BANKS) + 1))
                    for b in range(b0, b1):
                        mm = pe.transpose(ps[:, T_BANKS[u % len(T_BANKS)], P * (b - b0):P * (b - b0) + P],
                                          probs[:, n % P_BUFS, P * b:P * b + P], ident[:])
                    mm.then_inc(q["turned"], 1)

            def with_values(g, pair, n, j0, j1):
                m, step, c = chunk_after(n)
                a, latent = divmod(step, 2)
                last = 2 * c + 1
                half, first, _ = part_of_pt(n)
                if j0 == 0:
                    pe.wait_ge(q["pt_lo_made"], per_pair(g, pair, T_UNITS, UNITS_BEFORE[n + 1]))
                    if m >= len(O_BANKS):
                        pe.wait_ge(q["o_lo_made"], per_pair(g, pair, CHUNKS, m - len(O_BANKS) + 1))
                vals = [w[:, a] for w in (lv_hi, lv_lo)] if latent else [v_hi[:], v_lo[:]]
                for j in range(j0, j1):
                    q0 = P if j == last else 0
                    at = 256 * (first + j)
                    mm = three(ps[:, O_BANKS[m % len(O_BANKS)], 256 * (m % 2) + q0:256 * (m % 2) + 256], [w[:, j, :] for w in vals],
                               [w[:, half, at + q0:at + 256] for w in (pt_hi, pt_lo)], j == 0, j == last)
                if j1 == last + 1:
                    mm.then_inc(q["pv_mm"], 1)

            def outputs(g, pair, y):
                t = OUT_ORDER[y]
                pe.wait_ge(q["o_lo_made"], per_pair(g, pair, CHUNKS, 3 * ST // 2 + y // 2 + 1))
                if y >= 4:
                    pe.wait_ge(q["out_added"], SEED + per_pair(g, pair, ST, y - 3))
                for step in range(STEPS):
                    a, latent = divmod(step, 2)
                    lhs = [w[:, a, P * t:P * t + P] for w in ((ql_hi, ql_lo) if latent else (o_hi, o_lo))]
                    made, at = STEP_WEIGHTS[step]
                    if y == 0:
                        pe.wait_ge(q["wo_lo"], SEED + per_pair(g, pair, len(OUT_PARTS), made))
                    mm = three(ps[:, y % 4, :], lhs, [w[:, 1, at:at + D] for w in (pt_hi, pt_lo)],
                               step == 0, step == STEPS - 1)
                mm.then_inc(q["out_mm"], 1)

            pe.sem_inc(q["pv_mm"], SEED)
            pe.sem_inc(q["out_mm"], SEED)
            latent_query()
            pe.wait_ge(q["lq_lo_made"], 2)
            pe.wait_ge(q["const_made"], 6)
            with pe.Fori(0, GROUPS) as g:
                for pair in range(PAIRS):
                    for u in range(len(UNITS[pair])):
                        if u == len(UNITS[pair]) - 1:
                            for n in range(EARLY):
                                scores(g, pair, n)
                        unit(g, pair, u)
                        for r in turned_at(pair, u):
                            turn_roped(g, pair, r)
                    for k in range(SLOTS):
                        if EARLY <= k < TILES:
                            scores(g, pair, k)
                        for n, j0, j1 in PV_BEFORE.get(k, ()):
                            with_values(g, pair, n, j0, j1)
                        if 0 <= k - T_LAG < TILES:
                            turn_probs(g, pair, k - T_LAG)
                        for n, j0, j1 in PV_AFTER.get(k, ()):
                            with_values(g, pair, n, j0, j1)
                    for y in range(ST):
                        outputs(g, pair, y)

            ra = raw[:, 0, 0:CT * (E + E * R)].rearrange("p (c n) -> p c n", c=CT)
            for t in range(ST + 2):
                if t < ST:
                    pe.wait_ge(q["x1_made"], t + 1)
                    if t >= 2:
                        pe.wait_ge(q["x1T_made"], t - 1)
                    for c in range(CT):
                        mm = pe.transpose(ps[:, t % 2, P * c:P * c + P], acc[:, t, P * c:P * c + P], ident[:])
                    mm.then_inc(q["x1_turned"], 1)
                if t >= 2:
                    if t == 2:
                        pe.wait_ge(q["ffn_in"], 32)
                        pe.wait_ge(q["out_added"], SEED + GROUPS * PAIRS * ST)
                    pe.wait_ge(q["x1T_made"], t - 1)
                    for c in range(CT):
                        mm = pe.matmul(ps[:, 4 + (t - 2) // 2, 256 * (t % 2):256 * (t % 2) + E + E * R],
                                       probs[:].rearrange("p b n -> p (b n)")[:, 512 * ((t - 2) % 6) + P * c:512 * ((t - 2) % 6) + P * c + P],
                                       ra[:, c, :], start=c == 0 and t % 2 == 0, stop=c == CT - 1 and t % 2 == 1,
                                       skip_group_check=True)
                    mm.then_inc(q["logits_mm"], 1)
            for t in range(ST + 1):
                if t < ST:
                    pe.wait_ge(q["wh_made"], t + 1)
                    if t >= 2:
                        pe.wait_ge(q["whT_made"], t - 1)
                    pe.transpose(ps[:, t % 2, 0:P], raw[:, 2, P * t:P * t + P], ident[:]).then_inc(q["wh_turned"], 1)
                if t >= 1:
                    pe.wait_ge(q["whT_made"], t)
                    if t >= 3:
                        pe.wait_ge(q["y_added"], t - 2)
                    pe.matmul(ps[:, 2 + (t - 1) % 2, :], probs[:, 0, P * ((t - 1) % 2):P * ((t - 1) % 2) + P],
                              raw[:, 1, 0:D], start=True, stop=True).then_inc(q["y_mm"], 1)

        @block.scalar
        def _(act):
            def hi(dst, src):
                return nc.scalar.activation(dst, src, ACT.Copy)

            def weights_hi(g, name):
                load_landed(act, g, name)
                hi(parts(name)[0], raw_of(name)).then_inc(q["w_hi"], 1)

            def output_hi(g, pair, n):
                m, step, c = chunk_after(n)
                a, latent = divmod(step, 2)
                act.wait_ge(q["pv_mm"], SEED + per_pair(g, pair, CHUNKS, m + 1))
                hi((ql_hi if latent else o_hi)[:, a, 256 * c:256 * c + 256],
                   ps[:, O_BANKS[m % len(O_BANKS)], 256 * (m % 2):256 * (m % 2) + 256]).then_inc(q["o_hi_made"], 1)
                if m in OUT_AFTER:
                    part = OUT_AFTER.index(m)
                    if part < 2:
                        load_landed(act, g, f"{OUT_PARTS[part][0]}{pair}")
                    src, h, _ = output_weights(part, pair)
                    hi(h, src).then_inc(q["wo_hi"], 1)

            def probs_hi(g, pair, n):
                half, first, q0 = part_of_pt(n)
                dst = pt_hi[:, half, :].rearrange("p (j n) -> p j n", j=ST)
                for x, (b0, b1) in enumerate(blocks_of(n)):
                    u = UNITS_BEFORE[n] + x
                    act.wait_ge(q["turned"], per_pair(g, pair, T_UNITS, u + 1))
                    hi(dst[:, first + b0:first + b1, q0:q0 + P],
                       ps[:, T_BANKS[u % len(T_BANKS)], 0:P * (b1 - b0)].rearrange("p (j n) -> p j n", n=P)
                       ).then_inc(q["pt_hi_made"], 1)

            def exponentials(g, pair, n):
                act.wait_ge(q["maxed"], per_pair(g, pair, TILES, n + 1))
                if n >= P_BUFS:
                    act.wait_ge(q["turned"], per_pair(g, pair, T_UNITS, UNITS_BEFORE[n - P_BUFS + 1]))
                dst = probs[:, n % P_BUFS, 0:P * (ORDER[n % ST] + 1)]
                nc.scalar.activation(dst.rearrange("p (b n) -> p b n", b=len(SCORE_BANKS[n])), scores_of(n), ACT.Exp,
                                     bias=neg_max[:, n % 4:n % 4 + 1], scale=1.0,
                                     accum_out=row_sum[:, n % 4:n % 4 + 1]).then_inc(q["exped"], 1)

            xraw = acc[:].rearrange("p t n -> p (t n)").rearrange("p (c n) -> p c n", c=CT)
            act.wait_ge(q["wlq_in"], 16)
            hi(pt_hi[:, 0, 0:512], probs[:, 0, 0:512]).then_inc(q["wlq_hi_made"], 1)
            act.wait_ge(q["x_in"], 16)
            for c in range(CT):
                hi(x_hi[:, c, :], xraw[:, c, :]).then_inc(q["x_hi_made"], 1)
            for n in range(2):
                act.wait_ge(q["lq_mm"], n + 1)
                hi(lq_hi[:, 512 * n:512 * n + 512], ps[:, 4 + n, :]).then_inc(q["lq_hi_made"], 1)

            with act.Fori(0, GROUPS) as g:
                for pair in range(PAIRS):
                    act.wait_ge(q["pv_mm"], SEED + per_pair(g, pair, CHUNKS, 0))
                    act.wait_ge(q["wlk_in"], g * 32 + 16 * (pair + 1))
                    weights_hi(g, f"q{pair}")
                    hi(wlk_hi[:], wlk_raw[:]).then_inc(q["wlk_hi_made"], 1)
                    if pair == 0:
                        weights_hi(g, "kv")
                    act.wait_ge(q["out_mm"], SEED + per_pair(g, pair, ST, 0))
                    weights_hi(g, f"lv{pair}")

                    for u in range(len(UNITS[pair])):
                        if u == len(UNITS[pair]) - 1:
                            for n in range(EARLY_E):
                                exponentials(g, pair, n)
                        if u < len(UNITS[pair]):
                            kind, t = UNITS[pair][u]
                            bank = 4 + u % BANKS
                            if kind == "kv":
                                act.wait_ge(q["rope_mul"], rope_base(g, pair, u + 1))
                                hi(v_hi[:, t, :], ps[:, bank, P:2 * P]).then_inc(q["v_hi_made"], 1)
                            if kind == "lv":
                                act.wait_ge(q["lv_mm"], per_pair(g, pair, 4, t + 1))
                                hi(lv_hi[:, :, 2 * t:2 * t + 2, :].rearrange("p a t d -> p t a d"),
                                   ps[:, bank, :].rearrange("p (t a d) -> p t a d", t=2, a=2)).then_inc(q["lv_hi_made"], 1)
                        r = u - R_LAG
                        if 0 <= r < ROPES[pair]:
                            kind, t = UNITS[pair][r]
                            act.wait_ge(q["rope_t"], rope_base(g, pair, r + 1))
                            if kind == "ql":
                                hi(ql_hi[:, :, P * t:P * t + P],
                                   ps[:, r % 2, :].rearrange("p (a n) -> p a n", a=4)).then_inc(q["rope_hi"], 1)
                            else:
                                hi(k_hi[:, P * t:P * t + P], ps[:, r % 2, 0:P]).then_inc(q["rope_hi"], 1)

                    for k in range(SLOTS):
                        for op in ACT_ORDER:
                            if op == "o" and k in O_SLOT:
                                output_hi(g, pair, O_SLOT[k])
                            if op == "h" and 0 <= k - T_LAG - HL < TILES:
                                probs_hi(g, pair, k - T_LAG - HL)
                            if op == "e" and EARLY_E <= k < TILES:
                                exponentials(g, pair, k)

            def roots(signal, made):
                for half in range(2):
                    ts = slice(LN_TILES * half, LN_TILES * (half + 1))
                    act.wait_ge(q[signal], half + 1)
                    nc.scalar.activation(root[:, ts], ve[:, ts], ACT.Sqrt).then_inc(q[made], 1)

            roots("ve_made", "root_made")
            for t in range(ST):
                act.wait_ge(q["x1_turned"], t + 1)
                if t >= 6:
                    act.wait_ge(q["logits_mm"], t - 5)
                nc.scalar.activation(probs[:].rearrange("p b n -> p (b n)")[:, 512 * (t % 6):512 * (t % 6) + 512],
                                     ps[:, t % 2, :], ACT.Copy).then_inc(q["x1T_made"], 1)
            act.wait_ge(q["logits_mm"], ST)
            for t in range(ST):
                act.wait_ge(q["wh_turned"], t + 1)
                if t >= 2:
                    act.wait_ge(q["y_mm"], t - 1)
                nc.scalar.activation(probs[:, 0, P * (t % 2):P * (t % 2) + P], ps[:, t % 2, 0:P],
                                     ACT.Copy).then_inc(q["whT_made"], 1)
            roots("ve2_made", "root2_made")

        @block.gpsimd
        def _(pool):
            pool.sem_inc(q["w_lo_pool"], SEED)
            pool.sem_inc(q["wlk_lo_made"], SEED)
            chain = [0]

            def link(ins):
                chain[0] += 1
                ins.then_inc(q["const_made"], 1)
                pool.wait_ge(q["const_made"], chain[0])

            link(nc.gpsimd.memset(ident[:], 0.0))
            link(nc.gpsimd.affine_select(out=ident[:], in_=ident[:], compare_op=ALU.not_equal, fill=1.0, base=0,
                                         pattern=[[-1, P]], channel_multiplier=1))
            link(nc.gpsimd.tensor_copy(ident_b[:], ident[:]))
            link(nc.gpsimd.memset(mask_b[:], 0.0))
            link(nc.gpsimd.affine_select(out=mask_b[:], in_=mask_b[:], compare_op=ALU.is_ge, fill=MASKED, base=0,
                                         pattern=[[-1, P]], channel_multiplier=1))
            link(nc.gpsimd.iota(order[:], pattern=[[-1, E]], base=E, channel_multiplier=0,
                                allow_small_or_imprecise_dtypes=True))

            def weights_lo(g, name):
                pool.wait_ge(q["w_hi"], g * len(POOL_LO) + (POOL_LO.index(name) + 1))
                h, l = parts(name)
                nc.gpsimd.tensor_tensor(l, raw_of(name), h, ALU.subtract).then_inc(q["w_lo_pool"], 1)

            with pool.Fori(0, GROUPS) as g:
                for pair in range(PAIRS):
                    weights_lo(g, f"q{pair}")
                    pool.wait_ge(q["wlk_hi_made"], per_pair(g, pair, 1, 1))
                    nc.gpsimd.tensor_tensor(wlk_lo[:], wlk_raw[:], wlk_hi[:], ALU.subtract).then_inc(q["wlk_lo_made"], 1)
                    if pair == 0:
                        weights_lo(g, "kv")
                    weights_lo(g, f"lv{pair}")
                    for r in range(ROPES[pair]):
                        n = 4 * P if UNITS[pair][r][0] == "ql" else P
                        b = probs[:, r % P_BUFS, :]
                        pool.wait_ge(q["rope_mul"], rope_base(g, pair, r + 1))
                        nc.gpsimd.tensor_tensor(b[:, 0:n], b[:, 0:n], b[:, 512:512 + n], ALU.add).then_inc(q["rope_add"], 1)
                    for k in range(TILES):
                        w = P * (ORDER[k % ST] + 1)
                        b = probs[:, k % P_BUFS, 0:w]
                        pool.wait_ge(q["inverted"], per_pair(g, pair, TILES, k + 1))
                        nc.gpsimd.tensor_tensor(b, b, inv_sum[:, k % 4:k % 4 + 1].to_broadcast([P, w]),
                                                ALU.mult).then_inc(q["normed"], 1)

        @block.vector
        def _(dve):
            def lo(dst, src, h):
                return nc.vector.tensor_tensor(dst, src, h, ALU.subtract)

            dve.sem_inc(q["wo_lo"], SEED)
            dve.sem_inc(q["out_added"], SEED)
            xraw = acc[:].rearrange("p t n -> p (t n)").rearrange("p (c n) -> p c n", c=CT)
            dve.wait_ge(q["wlq_hi_made"], 1)
            lo(pt_lo[:, 0, 0:512], probs[:, 0, 0:512], pt_hi[:, 0, 0:512]).then_inc(q["wlq_lo_made"], 1)
            for c in range(CT):
                dve.wait_ge(q["x_hi_made"], c + 1)
                lo(x_lo[:, c, :], xraw[:, c, :], x_hi[:, c, :]).then_inc(q["x_lo_made"], 1)
            for n in range(2):
                dve.wait_ge(q["lq_hi_made"], n + 1)
                lo(lq_lo[:, 512 * n:512 * n + 512], ps[:, 4 + n, :], lq_hi[:, 512 * n:512 * n + 512]
                   ).then_inc(q["lq_lo_made"], 1)
            dve.wait_ge(q["tab_in"], 32)
            dve.wait_ge(q["res_in"], 16)

            def rope(g, pair, r):
                kind, t = UNITS[pair][r]
                if kind == "ql":
                    n = sum(k == "ql" for k, _ in UNITS[pair][:r + 1])
                    dve.wait_ge(q["ql_mm"], per_pair(g, pair, ST, n))
                else:
                    dve.wait_ge(q["kv_mm"], g * ST + (t + 1))
                h = 4 if kind == "ql" else 1
                src = ps[:, 4 + r % BANKS, 0:P * h].rearrange("p (h f d) -> p h f d", h=h, f=2)
                b = probs[:, r % P_BUFS, :]
                with_cos = b[:, 0:P * h].rearrange("p (h f d) -> p (h f) d", h=h, f=2)
                with_sin = b[:, 512:512 + P * h].rearrange("p (h f d) -> p h f d", h=h, f=2)
                c_t, s_t = cos_sb[:, t:t + 1, :], sin_sb[:, t:t + 1, :]
                nc.vector.tensor_tensor(with_cos, src.rearrange("p h f d -> p (h f) d"),
                                        c_t.to_broadcast([P, 2 * h, HALF]), ALU.mult)
                nc.vector.scalar_tensor_tensor(out=with_sin[:, :, 0, :], in0=src[:, :, 1, :], scalar=-1.0,
                                               in1=s_t.to_broadcast([P, h, HALF]), op0=ALU.mult, op1=ALU.mult)
                nc.vector.tensor_tensor(with_sin[:, :, 1, :], src[:, :, 0, :],
                                        s_t.to_broadcast([P, h, HALF]), ALU.mult).then_inc(q["rope_mul"], 1)

            def probs_lo(g, pair, n):
                half, first, q0 = part_of_pt(n)
                h, l = (w[:, half, :].rearrange("p (j n) -> p j n", j=ST) for w in (pt_hi, pt_lo))
                for x, (b0, b1) in enumerate(blocks_of(n)):
                    u = UNITS_BEFORE[n] + x
                    dve.wait_ge(q["pt_hi_made"], per_pair(g, pair, T_UNITS, u + 1))
                    lo(l[:, first + b0:first + b1, q0:q0 + P],
                       ps[:, T_BANKS[u % len(T_BANKS)], 0:P * (b1 - b0)].rearrange("p (j n) -> p j n", n=P),
                       h[:, first + b0:first + b1, q0:q0 + P]).then_inc(q["pt_lo_made"], 1)

            def row_max(g, pair, n):
                dve.wait_ge(q["scored"], per_pair(g, pair, TILES, n + 1))
                nc.vector.tensor_reduce(neg_max[:, n % 4:n % 4 + 1], scores_of(n), AX.XY, ALU.max,
                                        negate=True).then_inc(q["maxed"], 1)

            def inverse(g, pair, n):
                dve.wait_ge(q["exped"], per_pair(g, pair, TILES, n + 1))
                nc.vector.reciprocal(inv_sum[:, n % 4:n % 4 + 1], row_sum[:, n % 4:n % 4 + 1]
                                     ).then_inc(q["inverted"], 1)

            def output_lo(g, pair, n):
                m, step, c = chunk_after(n)
                a, latent = divmod(step, 2)
                h, l = (w[:, a, 256 * c:256 * c + 256] for w in ((ql_hi, ql_lo) if latent else (o_hi, o_lo)))
                dve.wait_ge(q["o_hi_made"], per_pair(g, pair, CHUNKS, m + 1))
                lo(l, ps[:, O_BANKS[m % len(O_BANKS)], 256 * (m % 2):256 * (m % 2) + 256], h).then_inc(q["o_lo_made"], 1)
                if m in OUT_AFTER:
                    part = OUT_AFTER.index(m)
                    src, h, l = output_weights(part, pair)
                    dve.wait_ge(q["wo_hi"], per_pair(g, pair, len(OUT_PARTS), part + 1))
                    lo(l, src, h).then_inc(q["wo_lo"], 1)

            with dve.Fori(0, GROUPS) as g:
                for pair in range(PAIRS):
                    for u in range(len(UNITS[pair]) + 1):
                        if u < ROPES[pair]:
                            rope(g, pair, u)
                        if u == len(UNITS[pair]):
                            for n in range(EARLY):
                                row_max(g, pair, n)
                        if 0 <= u - 1 < len(UNITS[pair]):
                            kind, t = UNITS[pair][u - 1]
                            bank = 4 + (u - 1) % BANKS
                            if kind == "kv":
                                dve.wait_ge(q["v_hi_made"], g * ST + (t + 1))
                                lo(v_lo[:, t, :], ps[:, bank, P:2 * P], v_hi[:, t, :]).then_inc(q["v_lo_made"], 1)
                            if kind == "lv":
                                dve.wait_ge(q["lv_hi_made"], per_pair(g, pair, 4, t + 1))
                                lo(lv_lo[:, :, 2 * t:2 * t + 2, :].rearrange("p a t d -> p t a d"),
                                   ps[:, bank, :].rearrange("p (t a d) -> p t a d", t=2, a=2),
                                   lv_hi[:, :, 2 * t:2 * t + 2, :].rearrange("p a t d -> p t a d")
                                   ).then_inc(q["lv_lo_made"], 1)
                        r = u - 3
                        if 0 <= r < ROPES[pair]:
                            kind, t = UNITS[pair][r]
                            dve.wait_ge(q["rope_hi"], rope_base(g, pair, r + 1))
                            if kind == "ql":
                                lo(ql_lo[:, :, P * t:P * t + P], ps[:, r % 2, :].rearrange("p (a n) -> p a n", a=4),
                                   ql_hi[:, :, P * t:P * t + P]).then_inc(q["rope_lo"], 1)
                            else:
                                lo(k_lo[:, P * t:P * t + P], ps[:, r % 2, 0:P], k_hi[:, P * t:P * t + P]
                                   ).then_inc(q["rope_lo"], 1)

                    for k in range(SLOTS):
                        for op in DVE_ORDER:
                            if op == "l" and 0 <= k - T_LAG - LL < TILES:
                                probs_lo(g, pair, k - T_LAG - LL)
                            if op == "m" and EARLY <= k < TILES:
                                row_max(g, pair, k)
                            if op == "r" and 0 <= k - 1 < TILES:
                                inverse(g, pair, k - 1)
                            if op == "o" and k - OL in O_SLOT:
                                output_lo(g, pair, O_SLOT[k - OL])

                    for y, t in enumerate(OUT_ORDER):
                        dve.wait_ge(q["out_mm"], SEED + per_pair(g, pair, ST, y + 1))
                        nc.vector.tensor_tensor(acc[:, t, :], ps[:, y % 4, :], acc[:, t, :], ALU.add
                                                ).then_inc(q["out_added"], 1)

            def link(name, count, ins):
                count[0] += 1
                ins.then_inc(q[name], 1)
                dve.wait_ge(q[name], count[0])

            def moments(name, count, t):
                link(name, count, nc.vector.bn_stats(stats[:, t, 0:6], acc[:, t, :]))
                link(name, count, nc.vector.bn_aggr(stats[:, t, 6:8], stats[:, t, 0:6]))

            def var_eps(half, signal):
                ts = slice(LN_TILES * half, LN_TILES * (half + 1))
                nc.vector.tensor_scalar(ve[:, ts], stats[:, ts, 7], EPS, None, ALU.add).then_inc(q[signal], 1)

            def inverse_root(name, count, half, signal):
                ts = slice(LN_TILES * half, LN_TILES * (half + 1))
                dve.wait_ge(q[signal], half + 1)
                link(name, count, nc.vector.reciprocal(rstd[:, ts], root[:, ts]))
                link(name, count, nc.vector.tensor_tensor(newton[:, ts], rstd[:, ts], rstd[:, ts], ALU.mult))
                link(name, count, nc.vector.tensor_tensor(newton[:, ts], newton[:, ts], ve[:, ts], ALU.mult))
                link(name, count, nc.vector.tensor_scalar(newton[:, ts], newton[:, ts], -0.5, 1.5, ALU.mult, ALU.add))
                link(name, count, nc.vector.tensor_tensor(rstd[:, ts], rstd[:, ts], newton[:, ts], ALU.mult))

            def finish(count, half):
                inverse_root("ln2_chain", count, half, "root2_made")
                for t in range(LN_TILES * half, LN_TILES * (half + 1)):
                    normalize(t).then_inc(q["finished"], 1)

            def normalize(t):
                return nc.vector.tensor_scalar(acc[:, t, :], acc[:, t, :], stats[:, t, 6:7], rstd[:, t:t + 1],
                                               ALU.subtract, ALU.mult)

            dve.wait_ge(q["out_added"], SEED + GROUPS * PAIRS * ST)
            ln = [0]
            for half in range(2):
                for t in range(LN_TILES * half, LN_TILES * (half + 1)):
                    moments("ln_chain", ln, t)
                var_eps(half, "ve_made")
            for half in range(2):
                inverse_root("ln_chain", ln, half, "root_made")
                for t in range(LN_TILES * half, LN_TILES * (half + 1)):
                    normalize(t).then_inc(q["x1_made"], 1)

            def step(ins):
                chain[0] += 1
                ins.then_inc(q["route_chain"], 1)
                dve.wait_ge(q["route_chain"], chain[0])

            chain = [0]
            dve.wait_ge(q["logits_mm"], ST)
            mix = ps[:, 4:8, :].rearrange("p b (y n) -> p (b y) n", y=2)
            logits, equal, ranked, first, weight = (route[:, i] for i in range(5))
            step(nc.vector.tensor_copy(logits, mix[:, :, 0:E]))
            step(nc.vector.tensor_reduce(top[:], logits, AX.X, ALU.max))
            step(nc.vector.tensor_tensor(equal, logits, top[:, :, None].to_broadcast([P, ST, E]), ALU.is_equal))
            step(nc.vector.tensor_tensor(ranked, equal, order[:, None, :].to_broadcast([P, ST, E]), ALU.mult))
            step(nc.vector.tensor_reduce(top2[:], ranked, AX.X, ALU.max))
            step(nc.vector.tensor_tensor(first, ranked, top2[:, :, None].to_broadcast([P, ST, E]), ALU.is_equal))
            step(nc.vector.tensor_tensor(weight, first, top[:, :, None].to_broadcast([P, ST, E]), ALU.mult))
            for t in range(ST):
                nc.vector.tensor_tensor(raw[:, 2, P * t:P * t + P].rearrange("p (e r) -> p e r", e=E),
                                        mix[:, t, E:E + E * R].rearrange("p (e r) -> p e r", e=E),
                                        weight[:, t, :, None].to_broadcast([P, E, R]), ALU.mult).then_inc(q["wh_made"], 1)
            ln2 = [0]
            for half in range(2):
                for t in range(LN_TILES * half, LN_TILES * (half + 1)):
                    dve.wait_ge(q["y_mm"], t + 1)
                    nc.vector.tensor_tensor(acc[:, t, :], ps[:, 2 + t % 2, :], acc[:, t, :], ALU.add
                                            ).then_inc(q["y_added"], 1)
                    dve.wait_ge(q["y_added"], t + 1)
                    moments("ln2_chain", ln2, t)
                var_eps(half, "ve2_made")
                if half == 1:
                    finish(ln2, 0)
            finish(ln2, 1)


def rope_tables():
    inv_freq = np.float32(1.0) / (10000.0 ** (np.arange(0, HD, 2) / HD)).astype(np.float32)
    angle = np.outer(np.arange(S, dtype=np.float32), inv_freq.astype(np.float32)).astype(np.float32)
    share = float(HD) ** -0.25
    tables = [(f(angle.astype(np.float64)) * share).astype(np.float32) for f in (np.cos, np.sin)]
    return [np.ascontiguousarray(t.reshape(ST, P, HALF).transpose(1, 0, 2)) for t in tables]


def kernel(**inputs):
    import concourse.bacc as bacc
    from concourse.bass_utils import run_bass_kernel_spmd

    a = {k.replace("L0_attn_", "").replace("L0_ffn_", ""): np.asarray(v) for k, v in inputs.items()}
    x = a["hidden_states"][0]

    def by_pair(w):
        return w.reshape(CT, P, GROUPS, PAIRS, 256).transpose(2, 3, 1, 0, 4).reshape(GROUPS, PAIRS, P, CT * 256)

    cos, sin = rope_tables()
    kv = np.stack([a[n].reshape(CT, P, GROUPS, HD) for n in ("w_k", "w_v")], axis=3)
    wo = np.stack([a[n].reshape(GROUPS, PAIRS, 2, HD, D) for n in ("w_o", "w_lo")], axis=4)
    arrays = {
        "xT": x.T.reshape(CT, P, S).transpose(1, 0, 2).reshape(P, CT * S),
        "x": x.reshape(ST, P, D).transpose(1, 0, 2),
        "wlq": a["w_lq"].reshape(CT, P, P).transpose(1, 0, 2).reshape(P, CT * P),
        "wq": by_pair(a["w_q"]),
        "wkv": kv.transpose(2, 1, 0, 3, 4).reshape(GROUPS, P, CT * 256),
        "wlk": a["w_lk"].reshape(P, GROUPS, PAIRS, 256).transpose(1, 2, 0, 3),
        "wlv": by_pair(a["w_lv"]),
        "wo": wo.transpose(0, 1, 2, 3, 4, 5).reshape(GROUPS, PAIRS, 2, P, 2 * D),
        "cos": cos,
        "sin": sin,
        "route_a": np.concatenate([a["route_w"], a["A"].reshape(E * R, D)]).T.reshape(CT, P, E + E * R)
                     .transpose(1, 0, 2).reshape(P, CT * (E + E * R)),
        "bwT": a["Bw"].transpose(0, 2, 1).reshape(E * R, D),
    }
    arrays = {k: np.ascontiguousarray(v) for k, v in arrays.items()}
    nc = bacc.Bacc("TRN2", target_bir_lowering=False, num_devices=1)
    args = [nc.dram_tensor(k, v.shape, F32, kind="ExternalInput").ap() for k, v in arrays.items()]
    out = nc.dram_tensor("out", (S, D), F32, kind="ExternalOutput").ap()
    block_kernel(nc, *args, out.rearrange("(t p) n -> p t n", p=P))
    r = run_bass_kernel_spmd(nc, [arrays], core_ids=[0])
    return r.results[0]["out"].reshape(1, S, D)
```
